# Optimizing a Trainium2 kernel written in Bass

```python
import numpy as np
import jax
import jax.numpy as jnp

def _softmax(x, axis=-1):
    return jax.nn.softmax(x, axis=axis)

def _gelu(x):
    return jax.nn.gelu(x, approximate=True)

def _silu(x):
    return jax.nn.silu(x)

def _sigmoid(x):
    return jax.nn.sigmoid(x)

def _layernorm(x, axis=-1, eps=1e-05):
    m = jnp.mean(x, axis=axis, keepdims=True)
    v = jnp.var(x, axis=axis, keepdims=True)
    return (x - m) / jnp.sqrt(v + eps)

def _scatter_add(tgt, idx, src, axis=0):
    return tgt.at[idx].add(src)

def _segment_sum(src, seg, n):
    return jax.ops.segment_sum(src, seg, n)
kernel_name = 'mk_decoder_preln_d1_seqx_r8_082837'

def setup_inputs(seed: int=0):
    np.random.seed(seed)
    _w = jnp.asarray

    def _rec_inputs():
        import jax
        import jax.numpy as jnp
        _rk = jax.random.key(seed)
        x = -0.0002928 + 1 * jax.random.normal(jax.random.fold_in(_rk, 1), (16, 128, 128), jnp.float32)
        _lenS = 128 - jax.random.randint(jax.random.fold_in(_rk, 7), (16,), 0, max(1, 128 // 4) + 1, jnp.int32)
        _lenS2 = 128 - jax.random.randint(jax.random.fold_in(_rk, 8), (16,), 0, max(1, 128 // 4) + 1, jnp.int32)
        _ctx_1024P = jax.random.normal(jax.random.fold_in(_rk, 11), (16, 16, 128), jnp.float32)
        _ctx_1024c = jax.random.dirichlet(jax.random.fold_in(_rk, 511), 0.3 * jnp.ones((16,), jnp.float32), (16, 128))
        _ctx_1024t = jnp.einsum('bsk,bkd->bsd', _ctx_1024c, _ctx_1024P)
        _ctx_1024t = _ctx_1024t * jax.lax.rsqrt(jnp.mean(jnp.square(_ctx_1024t)) + 1e-12) * 0.953939
        ctx_1024 = -1.39393e-06 + 0.999914 * (_ctx_1024t + 0.3 * jax.random.normal(jax.random.fold_in(_rk, 611), (16, 128, 128), jnp.float32))
        fside_BxS2_0 = jax.random.uniform(jax.random.fold_in(_rk, 12), (16, 128), jnp.float32, 0.0, 0.499917)
        itok_BxS2_0_7 = jax.random.randint(jax.random.fold_in(_rk, 14), (16, 128), 0, 8, jnp.int32)
        _validS = jnp.arange(128)[None, :] < _lenS[:, None]
        _validS2 = jnp.arange(128)[None, :] < _lenS2[:, None]
        _causal = jnp.tril(jnp.ones((128, 128), dtype=bool))
        mask_BxS2_bf0 = jnp.logical_not(jnp.ones((16, 128), dtype=bool))
        return (x, ctx_1024, fside_BxS2_0, itok_BxS2_0_7, mask_BxS2_bf0)
    x, ctx_1024, fside_BxS2_0, itok_BxS2_0_7, mask_BxS2_bf0 = _rec_inputs()

    def _L0_attn_setup():
        import jax, jax.numpy as jnp
        import numpy as np
        B, S, D = (1, 512, 128)
        H, W = (16, 64)
        HD = D // H
        key = jax.random.key(seed)
        k1, k2, k3 = jax.random.split(key, 3)
        x = jax.random.normal(k1, (B, S, D), dtype=jnp.float32)
        w_qkv = jax.random.normal(k2, (D, 3 * D), dtype=jnp.float32) * 0.02
        w_out = jax.random.normal(k3, (D, D), dtype=jnp.float32) * 0.02
        return {'x': x, 'w_qkv': w_qkv, 'w_out': w_out}
    _L0_attn_all = _L0_attn_setup()
    _L0_attn_in = {k: v for k, v in _L0_attn_all.items() if k in ('w_qkv', 'w_out')}
    del _L0_attn_all

    def _L0_xattn_setup():
        import math
        import jax, jax.numpy as jnp
        import numpy as np
        D_MODEL = 128
        NUM_HEADS = 16
        N_BUCKETS = 8
        B, L, S = (2, 256, 256)
        NEG_INF = -1e+30
        key = jax.random.key(seed)
        ks = jax.random.split(key, 12)
        inv = 1.0 / math.sqrt(D_MODEL)
        return {'query': jax.random.normal(ks[0], (B, L, D_MODEL), jnp.float32), 'key': jax.random.normal(ks[1], (B, S, D_MODEL), jnp.float32), 'value': jax.random.normal(ks[2], (B, S, D_MODEL), jnp.float32), 'query_times': jax.random.uniform(ks[3], (B, L), jnp.float32) * 0.5, 'key_times': jax.random.uniform(ks[4], (B, S), jnp.float32), 'key_padding_mask': jnp.zeros((B, S), dtype=bool), 'source_bucket_ids': jax.random.randint(ks[5], (B, S), 0, N_BUCKETS, jnp.int32), 'Wq': jax.random.normal(ks[6], (D_MODEL, D_MODEL), jnp.float32) * inv, 'Wk_b': jax.random.normal(ks[7], (N_BUCKETS, D_MODEL, D_MODEL), jnp.float32) * inv, 'Wv_b': jax.random.normal(ks[8], (N_BUCKETS, D_MODEL, D_MODEL), jnp.float32) * inv, 'Wo': jax.random.normal(ks[9], (D_MODEL, D_MODEL), jnp.float32) * inv, 'bo': jnp.zeros((D_MODEL,), jnp.float32)}
    _L0_xattn_all = _L0_xattn_setup()
    _L0_xattn_in = {k: v for k, v in _L0_xattn_all.items() if k in ('Wq', 'Wk_b', 'Wv_b', 'Wo', 'bo')}
    del _L0_xattn_all

    def _L0_ffn_setup():
        import jax, jax.numpy as jnp
        import numpy as np
        D = 128
        H = 4
        HD = D // H
        E = 8
        FF = 512
        CAP_FACTOR = 1.0

        def _ln(x, g, b, eps=1e-05):
            mu = jnp.mean(x, -1, keepdims=True)
            v = jnp.mean((x - mu) ** 2, -1, keepdims=True)
            return (x - mu) * jax.lax.rsqrt(v + eps) * g + b

        def _mha(x, w, b, ow, ob):
            L, N, _ = x.shape
            qkv = x @ w.T + b
            q, k, v = jnp.split(qkv, 3, axis=-1)
            rh = lambda t: t.reshape(L, N, H, HD).transpose(1, 2, 0, 3)
            q, k, v = (rh(q), rh(k), rh(v))
            scores = jnp.einsum('nhld,nhmd->nhlm', q, k) / np.float32(np.sqrt(HD))
            attn = jax.nn.softmax(scores, axis=-1)
            o = jnp.einsum('nhlm,nhmd->nhld', attn, v).transpose(2, 0, 1, 3).reshape(L, N, D)
            return o @ ow.T + ob

        def _moe(x, wg, w1, b1, w2, b2):
            L, N, _ = x.shape
            S = L * N
            cap = int(CAP_FACTOR * S) // E
            xf = x.reshape(S, D)
            gates = jax.nn.softmax(xf @ wg, axis=-1)
            idx = jnp.argmax(gates, axis=-1)
            mask1 = jax.nn.one_hot(idx, E, dtype=x.dtype)
            loc = jnp.sum((jnp.cumsum(mask1, 0) - 1.0) * mask1, -1).astype(jnp.int32)
            keep = loc < cap
            gate_val = jnp.take_along_axis(gates, idx[:, None], -1)[:, 0]
            slot = jnp.where(keep, idx.astype(jnp.int32) * cap + loc, E * cap)
            disp = jnp.zeros((E * cap, D), x.dtype).at[slot].set(xf, mode='drop')
            disp = disp.reshape(E, cap, D)
            h = jnp.einsum('ecd,edf->ecf', disp, w1) + b1[:, None, :]
            y = (jnp.einsum('ecf,efd->ecd', h, w2) + b2[:, None, :]).reshape(E * cap, D)
            out = jnp.where(keep[:, None], gate_val[:, None] * y[jnp.minimum(slot, E * cap - 1)], 0.0)
            return out.reshape(L, N, D)
        key = jax.random.key(seed)
        ks = jax.random.split(key, 8)
        L, N = (128, 16)
        s = 0.02
        return {'x': jax.random.normal(ks[0], (L, N, D), jnp.float32), 'in_proj_w': jax.random.normal(ks[1], (3 * D, D), jnp.float32) * s, 'in_proj_b': jnp.zeros((3 * D,), jnp.float32), 'out_proj_w': jax.random.normal(ks[2], (D, D), jnp.float32) * s, 'out_proj_b': jnp.zeros((D,), jnp.float32), 'ln1_g': jnp.ones((D,), jnp.float32), 'ln1_b': jnp.zeros((D,), jnp.float32), 'ln2_g': jnp.ones((D,), jnp.float32), 'ln2_b': jnp.zeros((D,), jnp.float32), 'wg': jax.random.normal(ks[3], (D, E), jnp.float32) * s, 'w1': jax.random.normal(ks[4], (E, D, FF), jnp.float32) * s, 'b1': jnp.zeros((E, FF), jnp.float32), 'w2': jax.random.normal(ks[5], (E, FF, D), jnp.float32) * s, 'b2': jnp.zeros((E, D), jnp.float32)}
    _L0_ffn_all = _L0_ffn_setup()
    _L0_ffn_in = {k: v for k, v in _L0_ffn_all.items() if k in ('in_proj_w', 'in_proj_b', 'out_proj_w', 'out_proj_b', 'ln1_g', 'ln1_b', 'ln2_g', 'ln2_b', 'wg', 'w1', 'b1', 'w2', 'b2')}
    del _L0_ffn_all
    return {'x': x, 'ctx_1024': ctx_1024, 'fside_BxS2_0': fside_BxS2_0, 'itok_BxS2_0_7': itok_BxS2_0_7, 'mask_BxS2_bf0': mask_BxS2_bf0, 'L0_attn_w_qkv': _L0_attn_in['w_qkv'], 'L0_attn_w_out': _L0_attn_in['w_out'], 'L0_xattn_Wq': _L0_xattn_in['Wq'], 'L0_xattn_Wk_b': _L0_xattn_in['Wk_b'], 'L0_xattn_Wv_b': _L0_xattn_in['Wv_b'], 'L0_xattn_Wo': _L0_xattn_in['Wo'], 'L0_xattn_bo': _L0_xattn_in['bo'], 'L0_ffn_in_proj_w': _L0_ffn_in['in_proj_w'], 'L0_ffn_in_proj_b': _L0_ffn_in['in_proj_b'], 'L0_ffn_out_proj_w': _L0_ffn_in['out_proj_w'], 'L0_ffn_out_proj_b': _L0_ffn_in['out_proj_b'], 'L0_ffn_ln1_g': _L0_ffn_in['ln1_g'], 'L0_ffn_ln1_b': _L0_ffn_in['ln1_b'], 'L0_ffn_ln2_g': _L0_ffn_in['ln2_g'], 'L0_ffn_ln2_b': _L0_ffn_in['ln2_b'], 'L0_ffn_wg': _L0_ffn_in['wg'], 'L0_ffn_w1': _L0_ffn_in['w1'], 'L0_ffn_b1': _L0_ffn_in['b1'], 'L0_ffn_w2': _L0_ffn_in['w2'], 'L0_ffn_b2': _L0_ffn_in['b2']}

def reference(x, ctx_1024, fside_BxS2_0, itok_BxS2_0_7, mask_BxS2_bf0, L0_attn_w_qkv, L0_attn_w_out, L0_xattn_Wq, L0_xattn_Wk_b, L0_xattn_Wv_b, L0_xattn_Wo, L0_xattn_bo, L0_ffn_in_proj_w, L0_ffn_in_proj_b, L0_ffn_out_proj_w, L0_ffn_out_proj_b, L0_ffn_ln1_g, L0_ffn_ln1_b, L0_ffn_ln2_g, L0_ffn_ln2_b, L0_ffn_wg, L0_ffn_w1, L0_ffn_b1, L0_ffn_w2, L0_ffn_b2):
    import jax
    import jax.numpy as jnp

    def _L0_attn_ref(x, w_qkv, w_out):
        import jax, jax.numpy as jnp
        import numpy as np
        B, S, D = (1, 512, 128)
        H, W = (16, 64)
        HD = D // H
        b, s, d = x.shape
        qkv = x @ w_qkv
        q, k, v = jnp.split(qkv, 3, axis=-1)
        to_heads = lambda t: t.reshape(b, s, H, HD).transpose(0, 2, 1, 3)
        q, k, v = map(to_heads, (q, k, v))
        C = s // W
        qc = q.reshape(b, H, C, W, HD)
        kc = k.reshape(b, H, C, W, HD)
        vc = v.reshape(b, H, C, W, HD)
        zero = jnp.zeros_like(kc[:, :, :1])
        k_prev = jnp.concatenate([zero, kc[:, :, :-1]], axis=2)
        v_prev = jnp.concatenate([jnp.zeros_like(vc[:, :, :1]), vc[:, :, :-1]], axis=2)
        kcat = jnp.concatenate([k_prev, kc], axis=3)
        vcat = jnp.concatenate([v_prev, vc], axis=3)
        scores = jnp.einsum('bhcqd,bhckd->bhcqk', qc, kcat) / HD ** 0.5
        wq = jnp.arange(W)
        jk = jnp.arange(2 * W)
        ci = jnp.arange(C)
        causal = wq[:, None] + W >= jk[None, :]
        valid = ci[:, None, None] * W + jk[None, None, :] - W >= 0
        mask = causal[None] & valid
        scores = jnp.where(mask[None, None], scores, -jnp.inf)
        attn = jax.nn.softmax(scores, axis=-1)
        out = jnp.einsum('bhcqk,bhckd->bhcqd', attn, vcat)
        out = out.reshape(b, H, s, HD).transpose(0, 2, 1, 3).reshape(b, s, d)
        return out @ w_out

    def _L0_xattn_ref(query, key, value, query_times, key_times, key_padding_mask, source_bucket_ids, Wq, Wk_b, Wv_b, Wo, bo):
        import math
        import jax, jax.numpy as jnp
        import numpy as np
        D_MODEL = 128
        NUM_HEADS = 16
        N_BUCKETS = 8
        B, L, S = (2, 256, 256)
        NEG_INF = -1e+30
        Bq, Lq, D = query.shape
        Sq = key.shape[1]
        H = NUM_HEADS
        dk = D // H
        Q = (query @ Wq).reshape(Bq, Lq, H, dk).transpose(0, 2, 1, 3)
        N = Bq * Sq
        kf = key.reshape(N, D)
        vf = value.reshape(N, D)
        buckets = source_bucket_ids.reshape(N)
        K_all = jnp.einsum('nd,edk->enk', kf, Wk_b)
        V_all = jnp.einsum('nd,edk->enk', vf, Wv_b)
        rows = jnp.arange(N)
        Kf = K_all[buckets, rows]
        Vf = V_all[buckets, rows]
        K = Kf.reshape(Bq, Sq, H, dk).transpose(0, 2, 1, 3)
        V = Vf.reshape(Bq, Sq, H, dk).transpose(0, 2, 1, 3)
        time_diff = query_times[:, :, None] - key_times[:, None, :]
        attend = (time_diff < 0)[:, None, :, :] | key_padding_mask[:, None, None, :]
        scores = jnp.einsum('bhld,bhsd->bhls', Q, K) / math.sqrt(dk)
        scores = jnp.where(attend, scores, NEG_INF)
        attn = jax.nn.softmax(scores, axis=-1)
        ctx = jnp.einsum('bhls,bhsd->bhld', attn, V)
        ctx = ctx.transpose(0, 2, 1, 3).reshape(Bq, Lq, D)
        return ctx @ Wo + bo

    def _L0_ffn_ref(x, in_proj_w, in_proj_b, out_proj_w, out_proj_b, ln1_g, ln1_b, ln2_g, ln2_b, wg, w1, b1, w2, b2):
        import jax, jax.numpy as jnp
        import numpy as np
        D = 128
        H = 4
        HD = D // H
        E = 8
        FF = 512
        CAP_FACTOR = 1.0

        def _ln(x, g, b, eps=1e-05):
            mu = jnp.mean(x, -1, keepdims=True)
            v = jnp.mean((x - mu) ** 2, -1, keepdims=True)
            return (x - mu) * jax.lax.rsqrt(v + eps) * g + b

        def _mha(x, w, b, ow, ob):
            L, N, _ = x.shape
            qkv = x @ w.T + b
            q, k, v = jnp.split(qkv, 3, axis=-1)
            rh = lambda t: t.reshape(L, N, H, HD).transpose(1, 2, 0, 3)
            q, k, v = (rh(q), rh(k), rh(v))
            scores = jnp.einsum('nhld,nhmd->nhlm', q, k) / np.float32(np.sqrt(HD))
            attn = jax.nn.softmax(scores, axis=-1)
            o = jnp.einsum('nhlm,nhmd->nhld', attn, v).transpose(2, 0, 1, 3).reshape(L, N, D)
            return o @ ow.T + ob

        def _moe(x, wg, w1, b1, w2, b2):
            L, N, _ = x.shape
            S = L * N
            cap = int(CAP_FACTOR * S) // E
            xf = x.reshape(S, D)
            gates = jax.nn.softmax(xf @ wg, axis=-1)
            idx = jnp.argmax(gates, axis=-1)
            mask1 = jax.nn.one_hot(idx, E, dtype=x.dtype)
            loc = jnp.sum((jnp.cumsum(mask1, 0) - 1.0) * mask1, -1).astype(jnp.int32)
            keep = loc < cap
            gate_val = jnp.take_along_axis(gates, idx[:, None], -1)[:, 0]
            slot = jnp.where(keep, idx.astype(jnp.int32) * cap + loc, E * cap)
            disp = jnp.zeros((E * cap, D), x.dtype).at[slot].set(xf, mode='drop')
            disp = disp.reshape(E, cap, D)
            h = jnp.einsum('ecd,edf->ecf', disp, w1) + b1[:, None, :]
            y = (jnp.einsum('ecf,efd->ecd', h, w2) + b2[:, None, :]).reshape(E * cap, D)
            out = jnp.where(keep[:, None], gate_val[:, None] * y[jnp.minimum(slot, E * cap - 1)], 0.0)
            return out.reshape(L, N, D)
        y1 = _ln(x + _mha(x, in_proj_w, in_proj_b, out_proj_w, out_proj_b), ln1_g, ln1_b)
        y2 = _ln(y1 + _moe(y1, wg, w1, b1, w2, b2), ln2_g, ln2_b)
        return y2
    x = x + _L0_attn_ref(_layernorm(x, axis=-1), L0_attn_w_qkv, L0_attn_w_out)
    x = x + _L0_xattn_ref(_layernorm(x, axis=-1), ctx_1024, ctx_1024, fside_BxS2_0, fside_BxS2_0, mask_BxS2_bf0, itok_BxS2_0_7, L0_xattn_Wq, L0_xattn_Wk_b, L0_xattn_Wv_b, L0_xattn_Wo, L0_xattn_bo)
    x = x + _L0_ffn_ref(_layernorm(x, axis=-1), L0_ffn_in_proj_w, L0_ffn_in_proj_b, L0_ffn_out_proj_w, L0_ffn_out_proj_b, L0_ffn_ln1_g, L0_ffn_ln1_b, L0_ffn_ln2_g, L0_ffn_ln2_b, L0_ffn_wg, L0_ffn_w1, L0_ffn_b1, L0_ffn_w2, L0_ffn_b2)
    return x

_drawn_inputs = setup_inputs


def setup_inputs(seed=0):
    import zlib

    import numpy as np

    out = dict(_drawn_inputs(seed))
    spreads = {'L0_xattn_bo': (0.0, 0.1),
     'L0_ffn_in_proj_b': (0.0, 0.638),
     'L0_ffn_out_proj_b': (0.0, 0.1),
     'L0_ffn_ln1_g': (1.0, 0.2),
     'L0_ffn_ln1_b': (0.0, 0.1),
     'L0_ffn_ln2_g': (1.0, 0.2),
     'L0_ffn_ln2_b': (0.0, 0.1),
     'L0_ffn_b1': (0.0, 0.8),
     'L0_ffn_b2': (0.0, 0.8)}
    factors = {'L0_attn_w_qkv': 5.696,
     'L0_attn_w_out': 5.526,
     'L0_ffn_in_proj_w': 8.0,
     'L0_ffn_out_proj_w': 4.293,
     'L0_ffn_wg': 5.265,
     'L0_ffn_w1': 6.892,
     'L0_ffn_w2': 6.366}
    for name, (base, spread) in spreads.items():
        noise = np.random.default_rng([zlib.crc32(name.encode()), seed]).standard_normal(out[name].shape)
        drawn = base * np.exp(spread * noise) if base else spread * noise
        out[name] = jnp.asarray(drawn.astype(out[name].dtype))
    for name, factor in factors.items():
        out[name] = (out[name] * factor).astype(out[name].dtype)
    return out
```

```python
import numpy as np
import concourse.bass as bass
from concourse import mybir
from contextlib import ExitStack

B, S, D = 16, 128, 128
H, HD = 16, 8
NBUCKET = 8
MH, MHD = 4, 32
E, FF = 8, 512
CAP = B * S // E
EPS = 1e-5
NEG = -float(2 ** 100)
QUADS = 4
LAGS = 5
PEEL = 6


def decoder_kernel(nc, x, ctxT, fside, fsideT, itok, pad, w_qkv, w_out, wq, wkv, wo, bo,
                   inw, inb, ow, ob, g1, be1, g2, be2, wg, w1t, b1t, w2, b2t,
                   c_ident, c_causal, c_samepos, c_before, c_rank, c_batchof, out):
    f32, f32r, bf16 = mybir.dt.float32, mybir.dt.float32r, mybir.dt.bfloat16
    ALU, ACT, AX = mybir.AluOpType, mybir.ActivationFunctionType, mybir.AxisListType
    FC = FF // 128
    T = 2 * B
    nloads = [0]
    NPOS = S // B

    st = ExitStack()
    with st:
        def sb(name, shape, dt=f32):
            return st.enter_context(nc.sbuf_tensor(name, shape, dt))

        def sem(name):
            return st.enter_context(nc.semaphore(name))

        w_qkv_sb = sb("w_qkv_sb", [128, 3 * D])
        w_out_sb = sb("w_out_sb", [128, 2, D])
        wq_sb = sb("wq_sb", [128, D])
        wkv_sb = sb("wkv_sb", [128, NBUCKET, 2 * D])
        bo_row = sb("bo_row", [1, D])
        ones_row = sb("ones_row", [1, 128])
        inw_sb = sb("inw_sb", [128, 3 * D])
        inb_col = sb("inb_col", [128, 3])
        ow_sb = sb("ow_sb", [128, D])
        ob_row = sb("ob_row", [1, D])
        ln_rows = sb("ln_rows", [128, 4, D])
        wg_sb = sb("wg_sb", [128, E])
        w1t_sb = sb("w1t_sb", [128, E, FC, D])
        w2_sb = sb("w2_sb", [128, E, FC, D])
        b1t_sb = sb("b1t_sb", [128, FC, E])
        b2t_sb = sb("b2t_sb", [128, E])
        ident = sb("ident", [128, 128])
        causal = sb("causal", [128, 128])
        samepos = sb("samepos", [128, 128])
        before = sb("before", [128, 128], bf16)
        ones_bf = sb("ones_bf", [128, 128], bf16)
        rank = sb("rank", [128, B, E])
        batchof = sb("batchof", [128, B])
        x_sb = sb("x_sb", [128, B, D])
        ctx_sb = sb("ctx_sb", [128, B, S])
        itok_i = sb("itok_i", [128, B, S], mybir.dt.int32)
        itok_bf = sb("itok_bf", [128, B, S], bf16)
        onehot = sb("onehot", [128, NBUCKET, B, S], bf16)
        tk = sb("tk", [128, B, S])
        tq = sb("tq", [128, B])
        pad_words = sb("pad_words", [128, B, S // 4], mybir.dt.int32)
        pad_big = sb("pad_big", [128, B, S])

        stats = sb("stats", [128, 6])
        mv = sb("mv", [128, 2])
        veps = sb("veps", [128, 1])
        minus_half = sb("minus_half", [128, 1])
        rstd = sb("rstd", [128, 1])
        xn = sb("xn", [128, D])
        xnT = sb("xnT", [128, S])
        cm = sb("cm", [128, 2, NBUCKET, S])
        qs = sb("qs", [128, H, 2, 2, HD])
        ks = sb("ks", [128, H, 2, 2, HD])
        q4 = sb("q4", [128, 2, QUADS, S], f32r)
        k4 = sb("k4", [128, 2, QUADS, S], f32r)
        vaug = sb("vaug", [128, 2, H, 32])
        p_sb = sb("p_sb", [128, 2, QUADS, QUADS, S])
        m_sb = sb("m_sb", [128, 2, QUADS, QUADS])
        pT = sb("pT", [128, 2, QUADS, QUADS, S])
        oT = sb("oT", [128, QUADS, S])
        rden = sb("rden", [128, QUADS, QUADS])
        o_sb = sb("o_sb", [128, D])
        ofT = sb("ofT", [128, S])


        free = onehot[:, :, :, :].rearrange("p e b s -> p (e b s)").bitcast(f32)
        spans = [free[:, i * B * S:(i + 1) * B * S].rearrange("p (b s) -> p b s", b=B) for i in range(4)]
        y0T, qT, kT, aT = spans
        y0 = itok_i[:, :, :].bitcast(f32)
        y1 = tk[:, :, :]
        y1T = pad_big[:, :, :]
        vM = ctx_sb[:, :, :]
        prod = pT[:, :, :, :, :].rearrange("p u j r q -> p u (j r q)")[:, :, 0:E * D]\
            .rearrange("p u (e d) -> p u e d", e=E)
        mexp = sb("mexp", [128, E, D])
        cT = sb("cT", [128, E])
        cblk = p_sb[:, 0, :, :, :].rearrange("p j r k -> p (j r) k")
        crepT = sb("crepT", [128, B, E])
        crep = sb("crep", [128, D])
        st16 = sb("st16", [128, B, 6])
        mv16 = sb("mv16", [128, B, 2])
        ve16 = sb("ve16", [128, B])
        half16 = sb("half16", [128, B])
        rs16 = sb("rs16", [128, B])
        dsum = sb("dsum", [128, 4 * MH, QUADS])
        drec = sb("drec", [128, 4 * MH, QUADS])
        lg = sb("lg", [128, B, E])
        r_a = sb("r_a", [128, B, E])
        r_b = sb("r_b", [128, B, E])
        r_m = sb("r_m", [128, B])
        r_s = sb("r_s", [128, B])
        pick = sb("pick", [128, B, E])
        cum = sb("cum", [128, B + 1, E])
        pick_bf = sb("pick_bf", [128, B, E], bf16)
        cum_bf = sb("cum_bf", [128, B, E], bf16)
        gk = sb("gk", [128, B, E])
        gkT = sb("gkT", [128, 128])
        st2 = sb("st2", [128, 2, 6])
        mv2 = sb("mv2", [128, 2, 2])
        ve2 = sb("ve2", [128, 2])
        rs2 = sb("rs2", [128, 2])
        z = sb("z", [128, 2, D])
        w = sb("w", [128, 2, D])

        ps = st.enter_context(nc.psum_tensor("ps", [128, 8, 512], f32))
        bank = [ps[:, i, :] for i in range(8)]
        quad = [b.rearrange("p (r k) -> p r k", r=QUADS) for b in bank]

        names = """consts_in x_in attn_w_in ctx_in xw_in ffn_w_in ones_ready bn_step veps_ready pow_done xn_ready
            xT_done xnT_copied qkv_done hi_done split_done v_copied q4T_done q4_copied k4T_done k4_copied
            s_done added maxed subbed exped pT_done pT_copied pv_done oT_copied o4_done den_done o_ready
            fT_done fT_copied proj_done resid_done onehot_step mask_step cm_ready stored
            m_done m_copied cT_done cT_ready crepT_ready crep_done crep_copied st_step mv_step ve_ready rs_ready
            y0_ready f_xT_done f_xT_copied qk_done qT_ready kT_ready v_done v_ready f_s_done f_added f_maxed
            f_subbed f_exped f_sum f_drec f_divided f_pT_done f_pT_copied f_pv_done aT_ready f_proj_done
            z_ready w_ready wg_step y1_ready y1T_done y1T_copied logits_done route_step shifted gexp_ready
            cum_ready place_done gk_ready gkT_done gkT_copied cblk_ready xb_ready ffn_done bias_done gated
            tree_step tree_done y2_stats y2_w out_rows""".split()
        assert len(names) == len(set(names))
        s = {n: sem(n) for n in names}
        block = st.enter_context(nc.Block())

        def late(k, n=0):
            return not isinstance(k, int) or n <= k < T

        def layer_of(k, layer):
            return layer if not isinstance(k, int) else int(k >= B)

        def batch(k, layer):
            return k - B if layer_of(k, layer) else k

        def pipeline(e, step):
            for layer in range(2):
                for t in range(layer * B, layer * B + PEEL):
                    step(t, t % 2, layer)
                with e.Fori((layer * B + PEEL) // 2, (layer + 1) * B // 2) as i:
                    step(2 * i, 0, layer)
                    step(2 * i + 1, 1, layer)
            for t in range(T, T + LAGS):
                step(t, t % 2, 1)

        def bcast(v):
            return v[:, :].unsqueeze(2).broadcast_to([128, B, E])


        @block.sync
        def _(sp):
            sp.dma_start(x_sb[:, 0:4, :], x[0:4].rearrange("b s d -> s b d")).then_inc(s["x_in"], 16)
            sp.dma_start(ident[:, :], c_ident).then_inc(s["consts_in"], 16)
            sp.dma_start(w_qkv_sb[:, :], w_qkv).then_inc(s["attn_w_in"], 16)
            sp.dma_start(causal[:, :], c_causal).then_inc(s["consts_in"], 16)
            sp.dma_start(x_sb[:, 4:B, :], x[4:B].rearrange("b s d -> s b d")).then_inc(s["x_in"], 16)
            sp.dma_start(w_out_sb[:, 0, :], w_out).then_inc(s["attn_w_in"], 16)
            sp.dma_start(itok_i[:, :, :], itok.partition_broadcast(128)).then_inc(s["ctx_in"], 16)
            sp.dma_start(pad_words[:, :, :], pad.partition_broadcast(128)).then_inc(s["ctx_in"], 16)
            sp.dma_start(ctx_sb[:, :, :], ctxT.rearrange("b d s -> d b s")).then_inc(s["ctx_in"], 16)
            sp.dma_start(tk[:, :, :], fside.partition_broadcast(128)).then_inc(s["ctx_in"], 16)
            sp.dma_start(tq[:, :], fsideT).then_inc(s["ctx_in"], 16)
            sp.dma_start(wq_sb[:, :], wq).then_inc(s["xw_in"], 16)
            sp.dma_start(wkv_sb[:, :, :], wkv.rearrange("e d n -> d e n")).then_inc(s["xw_in"], 16)
            sp.dma_start(w_out_sb[:, 1, :], wo).then_inc(s["xw_in"], 16)
            sp.dma_start(bo_row[:, :], bo).then_inc(s["xw_in"], 16)
            loads = [(w1t_sb[:, :, :, :], w1t.rearrange("e (c p) d -> p e c d", p=128)),
                     (w2_sb[:, :, :, :], w2.rearrange("e (c p) d -> p e c d", p=128)),
                     (b1t_sb[:, :, :], b1t.rearrange("(c p) e -> p c e", p=128)), (b2t_sb[:, :], b2t),
                     (inw_sb[:, :], inw), (inb_col[:, :], inb), (ow_sb[:, :], ow), (ob_row[:, :], ob),
                     (wg_sb[:, :], wg), (samepos[:, :], c_samepos), (before[:, :], c_before),
                     (rank[:, :, :], c_rank), (batchof[:, :], c_batchof)]
            loads += [(ln_rows[:, i, :], v.partition_broadcast(128)) for i, v in enumerate((g1, be1, g2, be2))]
            for dst, src in loads:
                sp.dma_start(dst, src).then_inc(s["ffn_w_in"], 16)
            nloads[0] = len(loads)
            sp.wait_ge(s["out_rows"], B)
            sp.dma_start(out.rearrange("b s d -> s b d"), y0).then_inc(s["stored"], 16)
            sp.wait_ge(s["stored"], 16)

        @block.vector
        def _(dve):
            dve.memset(ones_row[:, :], 1.0).then_inc(s["ones_ready"], 1)
            dve.memset(vaug[:, :, :, :], 1.0).then_inc(s["ones_ready"], 1)
            dve.memset(minus_half[:, :], -0.5).then_inc(s["ones_ready"], 1)
            dve.memset(half16[:, :], -0.5).then_inc(s["ones_ready"], 1)
            dve.memset(ones_bf[:, :], 1.0).then_inc(s["ones_ready"], 1)
            dve.wait_ge(s["x_in"], 32)

            def norm_stats(t, layer):
                dve.bn_stats(stats[:, :], x_sb[:, batch(t, layer), :]).then_inc(s["bn_step"], 1)

            def norm_variance(t):
                if isinstance(t, int):
                    dve.wait_ge(s["bn_step"], 2 * t + 1)
                    if t >= 1:
                        dve.wait_ge(s["xn_ready"], t)
                dve.bn_aggr(mv[:, :], stats[:, :]).then_inc(s["bn_step"], 1)
                dve.wait_ge(s["bn_step"], 2 * t + 2)
                if late(t, 1):
                    dve.wait_ge(s["pow_done"], t)
                dve.tensor_scalar(veps[:, :], mv[:, 1:2], EPS, None, ALU.add).then_inc(s["veps_ready"], 1)

            def norm_rows(t, layer):
                dve.wait_ge(s["pow_done"], t + 1)
                if late(t, 1):
                    dve.wait_ge(s["xT_done"], t)
                dve.tensor_scalar(xn[:, :], x_sb[:, batch(t, layer), :], mv[:, 0:1], rstd[:, :],
                                  ALU.subtract, ALU.mult).then_inc(s["xn_ready"], 1)

            def split(h):
                dve.wait_ge(s["qkv_done"], h + 1)
                heads = bank[0][:, 0:2 * D].rearrange("p (a h d) -> p a h d", a=2, d=HD)
                q, k = (heads[:, i, :, :].unsqueeze(2).broadcast_to([128, H, 2, HD]) for i in range(2))
                if late(h, 1):
                    dve.wait_ge(s["k4T_done"], h)
                dve.tensor_copy(qs[:, :, :, 0, :].bitcast(f32r), q).then_inc(s["hi_done"], 1)
                dve.tensor_copy(ks[:, :, 0, :, :].bitcast(f32r), k).then_inc(s["hi_done"], 1)
                dve.wait_ge(s["hi_done"], 2 * h + 1)
                dve.tensor_tensor(qs[:, :, :, 1, :], q, qs[:, :, :, 0, :], ALU.subtract).then_inc(s["split_done"], 1)
                dve.wait_ge(s["hi_done"], 2 * h + 2)
                dve.tensor_tensor(ks[:, :, 1, :, :], k, ks[:, :, 0, :, :], ALU.subtract).then_inc(s["split_done"], 1)

            def unit(c, j, u, layer):
                mask = tk[:, batch(c, layer), :] if layer_of(c, layer) else causal[:, :]
                if isinstance(c, int) and c == B and j == 0:
                    dve.wait_ge(s["mask_step"], 4)
                if j == 0 and late(c, 2):
                    dve.wait_ge(s["pT_done"], 4 * c - 4)
                dve.wait_ge(s["s_done"], 4 * c + j + 1)
                dve.tensor_tensor(p_sb[:, u, j, :, :], quad[2 + j % 2],
                                  mask.unsqueeze(1).broadcast_to([128, QUADS, S]), ALU.add)\
                   .then_inc(s["added"], 1)
                dve.wait_ge(s["added"], 4 * c + j + 1)
                dve.tensor_reduce(m_sb[:, u, j, :], p_sb[:, u, j, :, :], AX.X, ALU.max).then_inc(s["maxed"], 1)

            def divide(o):
                dve.wait_ge(s["o4_done"], o + 1)
                o4 = bank[7].rearrange("p (r j c) -> p r j c", r=QUADS, j=QUADS)
                dve.reciprocal(rden[:, :, :], o4[:, :, :, HD]).then_inc(s["den_done"], 1)
                dve.wait_ge(s["den_done"], o + 1)
                if late(o, 1):
                    dve.wait_ge(s["fT_done"], o)
                dve.tensor_tensor(o_sb[:, :].rearrange("p (r j c) -> p r j c", r=QUADS, j=QUADS),
                                  o4[:, :, :, 0:HD],
                                  rden[:, :, :].unsqueeze(3).broadcast_to([128, QUADS, QUADS, HD]),
                                  ALU.mult).then_inc(s["o_ready"], 1)

            def residual(f, layer):
                dve.wait_ge(s["proj_done"], f + 1)
                rows = x_sb[:, batch(f, layer), :]
                dve.tensor_tensor(rows, rows, bank[1][:, 128:256], ALU.add).then_inc(s["resid_done"], 1)

            def buckets(e0, e1):
                for e in range(e0, e1):
                    dve.tensor_scalar(onehot[:, e, :, :], itok_bf[:, :, :], float(e), None, ALU.is_equal)\
                       .then_inc(s["onehot_step"], 1)

            def step(t, u, layer):
                h, c, o, f = t - 1, t - 2, t - 4, t - 5
                if late(t):
                    norm_stats(t, layer)
                if late(c):
                    unit(c, 0, u, layer)
                if late(t):
                    norm_variance(t)
                if late(h):
                    split(h)
                if late(c):
                    unit(c, 1, u, layer)
                if late(f):
                    residual(f, layer)
                if late(t):
                    norm_rows(t, layer)
                if late(c):
                    unit(c, 2, u, layer)
                if late(o):
                    divide(o)
                if late(c):
                    unit(c, 3, u, layer)
                if isinstance(t, int) and t == 2:
                    dve.wait_ge(s["ctx_in"], 16 * 5)
                    dve.tensor_copy(itok_bf[:, :, :], itok_i[:, :, :]).then_inc(s["onehot_step"], 1)
                    dve.tensor_scalar(pad_big[:, :, :], pad_words[:, :, :].bitcast(mybir.dt.uint8), -NEG, None, ALU.mult)\
                       .then_inc(s["onehot_step"], 1)
                    dve.wait_ge(s["onehot_step"], 1)
                if isinstance(t, int) and t in (3, 4):
                    buckets(4 * (t - 3), 4 * (t - 2))

            pipeline(dve, step)
            dve.wait_ge(s["ffn_w_in"], 16 * nloads[0])
            dve.wait_ge(s["cT_done"], 1)
            dve.tensor_tensor(cT[:, :], bank[4][:, 0:E], b2t_sb[:, :], ALU.add).then_inc(s["cT_ready"], 1)
            dve.wait_ge(s["cT_ready"], 1)
            dve.tensor_copy(crepT[:, :, :], cT[:, :].unsqueeze(1).broadcast_to([128, B, E])).then_inc(s["crepT_ready"], 1)
            dve.wait_ge(s["resid_done"], T)
            with dve.Fori(0, B) as b:
                dve.bn_stats(st16[:, b, :], x_sb[:, b, :]).then_inc(s["st_step"], 1)
            dve.wait_ge(s["st_step"], B)
            for b in range(B):
                dve.bn_aggr(mv16[:, b, :], st16[:, b, :]).then_inc(s["mv_step"], 1)
            dve.wait_ge(s["mv_step"], B)
            dve.tensor_scalar(ve16[:, :], mv16[:, :, 1], EPS, None, ALU.add).then_inc(s["ve_ready"], 1)
            dve.wait_ge(s["rs_ready"], 1)
            with dve.Fori(0, B) as b:
                dve.tensor_scalar(y0[:, b, :], x_sb[:, b, :], mv16[:, b, 0:1], rs16[:, bass.ds(b, 1)],
                                  ALU.subtract, ALU.mult).then_inc(s["y0_ready"], 1)
            dve.wait_ge(s["f_xT_copied"], 4)
            for i in range(4):
                dve.wait_ge(s["qk_done"], 2 * i + 2)
                dve.tensor_scalar(kT[:, 4 * i:4 * i + 4, :], quad[2 * (i % 2) + 1], inb_col[:, 1:2], None, ALU.add)\
                   .then_inc(s["kT_ready"], 1)

            def mha_sum(n):
                dve.wait_ge(s["f_exped"], n + 1)
                dve.tensor_reduce(dsum[:, n, :], p_sb[:, (n // 4) % 2, n % 4, :, :], AX.X, ALU.add).then_inc(s["f_sum"], 1)
                dve.wait_ge(s["f_sum"], n + 1)
                dve.reciprocal(drec[:, n, :], dsum[:, n, :]).then_inc(s["f_drec"], 1)

            def variances(i, k):
                for u in range(2):
                    dve.bn_aggr(mv2[:, u, :], st2[:, u, :]).then_inc(s["mv_step"], 1)
                    dve.wait_ge(s["mv_step"], B * (k + 1) + 2 * i + u + 1)
                    dve.tensor_scalar(ve2[:, u:u + 1], mv2[:, u, 1:2], EPS, None, ALU.add).then_inc(s["veps_ready"], 1)

            for n in range(4 * MH):
                scores = p_sb[:, (n // 4) % 2, n % 4, :, :]
                if n >= 8:
                    dve.wait_ge(s["f_pT_done"], n - 7)
                dve.wait_ge(s["f_s_done"], n + 1)
                dve.tensor_tensor(scores, quad[n % 4], samepos[:, :].unsqueeze(1).broadcast_to([128, QUADS, 128]), ALU.add)\
                   .then_inc(s["f_added"], 1)
                dve.wait_ge(s["f_added"], n + 1)
                dve.tensor_reduce(m_sb[:, (n // 4) % 2, n % 4, :], scores, AX.X, ALU.max).then_inc(s["f_maxed"], 1)
                if n >= 1:
                    mha_sum(n - 1)
            mha_sum(4 * MH - 1)
            with dve.Fori(0, B // 2) as i:
                for u in range(2):
                    b = 2 * i + u
                    dve.wait_ge(s["f_proj_done"], b + 1)
                    dve.tensor_tensor(z[:, u, :], y0[:, b, :], bank[6 + u][:, 0:D], ALU.add).then_inc(s["z_ready"], 1)
                    dve.wait_ge(s["z_ready"], b + 1)
                    dve.bn_stats(st2[:, u, :], z[:, u, :]).then_inc(s["st_step"], 1)
                variances(i, 0)
                for u in range(2):
                    b = 2 * i + u
                    dve.wait_ge(s["pow_done"], T + b + 1)
                    dve.tensor_scalar(w[:, u, :], z[:, u, :], mv2[:, u, 0:1], rs2[:, u:u + 1], ALU.subtract, ALU.mult)\
                       .then_inc(s["w_ready"], 1)
                    dve.wait_ge(s["w_ready"], b + 1)
                    dve.tensor_tensor(w[:, u, :], w[:, u, :], ln_rows[:, 0, :], ALU.mult).then_inc(s["wg_step"], 1)
                    dve.wait_ge(s["wg_step"], b + 1)
                    dve.tensor_tensor(y1[:, b, :], w[:, u, :], ln_rows[:, 1, :], ALU.add).then_inc(s["y1_ready"], 1)

            routed = [0]

            def route(ins):
                routed[0] += 1
                ins.then_inc(s["route_step"], 1)
                dve.wait_ge(s["route_step"], routed[0])

            dve.wait_ge(s["logits_done"], B)
            route(dve.tensor_copy(lg[:, :, :], bank[3][:, 0:B * E].rearrange("p (b e) -> p b e", e=E)))
            route(dve.tensor_reduce(r_m[:, :], lg[:, :, :], AX.X, ALU.max))
            dve.tensor_tensor(r_a[:, :, :], lg[:, :, :], bcast(r_m), ALU.subtract).then_inc(s["shifted"], 1)
            dve.wait_ge(s["shifted"], 1)
            route(dve.tensor_tensor(r_b[:, :, :], lg[:, :, :], bcast(r_m), ALU.is_equal))
            route(dve.tensor_tensor(r_b[:, :, :], r_b[:, :, :], rank[:, :, :], ALU.mult))
            route(dve.tensor_reduce(r_m[:, :], r_b[:, :, :], AX.X, ALU.max))
            route(dve.tensor_tensor(pick[:, :, :], r_b[:, :, :], bcast(r_m), ALU.is_equal))
            route(dve.tensor_copy(pick_bf[:, :, :], pick[:, :, :]))
            route(dve.memset(cum[:, 0, :], 0.0))
            for b in range(B):
                route(dve.tensor_tensor(cum[:, b + 1, :], cum[:, b, :], pick[:, b, :], ALU.add))
            dve.tensor_copy(cum_bf[:, :, :], cum[:, 0:B, :]).then_inc(s["cum_ready"], 1)
            dve.wait_ge(s["gexp_ready"], 1)
            route(dve.tensor_reduce(r_s[:, :], lg[:, :, :], AX.X, ALU.add))
            route(dve.reciprocal(r_m[:, :], r_s[:, :]))
            route(dve.tensor_tensor(gk[:, :, :], pick[:, :, :], bcast(r_m), ALU.mult))
            dve.wait_ge(s["place_done"], 1)
            route(dve.tensor_scalar(r_b[:, :, :], bank[2][:, 0:B * E].rearrange("p (b e) -> p b e", e=E), float(CAP), None,
                                    ALU.is_lt))
            dve.tensor_tensor(gk[:, :, :], gk[:, :, :], r_b[:, :, :], ALU.mult).then_inc(s["gk_ready"], 1)
            dve.wait_ge(s["gk_ready"], 1)
            dve.wait_ge(s["xb_ready"], 1)
            with dve.Fori(0, B // 2) as i:
                for u in range(2):
                    b = 2 * i + u
                    dve.wait_ge(s["ffn_done"], b + 1)
                    dve.tensor_tensor(prod[:, u, :, :], ps[:, 2 * u:2 * u + 2, :].rearrange("p a (e d) -> p (a e) d", d=D),
                                      gk[:, b, :].unsqueeze(2).broadcast_to([128, E, D]), ALU.mult)\
                       .then_inc(s["gated"], 1)
                    dve.wait_ge(s["tree_done"], b + 1)
                    dve.wait_ge(s["bias_done"], b + 1)
                    dve.tensor_tensor(z[:, u, :], prod[:, u, 0, :], bank[6 + u][:, 0:D], ALU.add).then_inc(s["z_ready"], 1)
                    dve.wait_ge(s["z_ready"], B + 2 * b + 1)
                    dve.tensor_tensor(z[:, u, :], z[:, u, :], y1[:, b, :], ALU.add).then_inc(s["z_ready"], 1)
                    dve.wait_ge(s["z_ready"], B + 2 * b + 2)
                    dve.bn_stats(st2[:, u, :], z[:, u, :]).then_inc(s["st_step"], 1)
                variances(i, 1)
                for u in range(2):
                    b = 2 * i + u
                    dve.wait_ge(s["pow_done"], T + B + b + 1)
                    dve.tensor_scalar(w[:, u, :], z[:, u, :], mv2[:, u, 0:1], rs2[:, u:u + 1], ALU.subtract, ALU.mult)\
                       .then_inc(s["w_ready"], 1)
                    dve.wait_ge(s["w_ready"], B + b + 1)
                    dve.tensor_tensor(w[:, u, :], w[:, u, :], ln_rows[:, 2, :], ALU.mult).then_inc(s["wg_step"], 1)
                    dve.wait_ge(s["wg_step"], B + b + 1)
                    dve.tensor_tensor(y0[:, b, :], w[:, u, :], x_sb[:, b, :], ALU.add).then_inc(s["out_rows"], 1)

        @block.gpsimd
        def _(pool):
            pool.wait_ge(s["ones_ready"], 5)

            def mask_part(part):
                if part == 0:
                    pool.wait_ge(s["ctx_in"], 16 * 5)
                    ins = pool.tensor_tensor(tk[:, :, :], tk[:, :, :],
                                             tq[:, :].unsqueeze(2).broadcast_to([128, B, S]), ALU.subtract)
                else:
                    pool.wait_ge(s["mask_step"], part)
                if part == 1:
                    ins = pool.tensor_scalar(tk[:, :, :], tk[:, :, :], 0.0, -NEG, ALU.is_gt, ALU.mult)
                if part == 2:
                    pool.wait_ge(s["onehot_step"], 2)
                    ins = pool.tensor_tensor(tk[:, :, :], tk[:, :, :], pad_big[:, :, :], ALU.add)
                if part == 3:
                    ins = pool.tensor_scalar(tk[:, :, :], tk[:, :, :], -NEG, 0.0, ALU.subtract, ALU.min)
                ins.then_inc(s["mask_step"], 1)

            def bucket_ctx(t, u):
                b = t - B
                if not isinstance(t, int) or t >= B + 2:
                    pool.wait_ge(s["qkv_done"], t - 1)
                if isinstance(t, int) and t == B:
                    pool.wait_ge(s["onehot_step"], NBUCKET + 2)
                pool.tensor_tensor(cm[:, u, :, :], onehot[:, :, b, :],
                                   ctx_sb[:, b, :].unsqueeze(1).broadcast_to([128, NBUCKET, S]),
                                   ALU.mult).then_inc(s["cm_ready"], 1)

            def unit(c, j, u):
                pool.wait_ge(s["maxed"], 4 * c + j + 1)
                pool.tensor_tensor(p_sb[:, u, j, :, :], p_sb[:, u, j, :, :],
                                   m_sb[:, u, j, :].unsqueeze(2).broadcast_to([128, QUADS, S]),
                                   ALU.subtract).then_inc(s["subbed"], 1)

            def step(t, u, layer):
                c = t - 2
                if late(t):
                    pool.wait_ge(s["veps_ready"], t + 1)
                    if late(t, 1):
                        pool.wait_ge(s["xn_ready"], t)
                    pool.tensor_tensor(rstd[:, :], veps[:, :], minus_half[:, :], ALU.pow)\
                        .then_inc(s["pow_done"], 1)
                if late(c):
                    unit(c, 0, u)
                    unit(c, 1, u)
                if late(t) and layer_of(t, layer):
                    bucket_ctx(t, u)
                if late(c):
                    unit(c, 2, u)
                if isinstance(t, int) and 2 <= t < 6:
                    mask_part(t - 2)
                if late(c):
                    unit(c, 3, u)

            pipeline(pool, step)
            pool.wait_ge(s["ve_ready"], 1)
            pool.tensor_tensor(rs16[:, :], ve16[:, :], half16[:, :], ALU.pow).then_inc(s["rs_ready"], 1)

            def mha_divide(n):
                p_unit = p_sb[:, (n // 4) % 2, n % 4, :, :]
                pool.wait_ge(s["f_drec"], n + 1)
                pool.tensor_tensor(p_unit, p_unit, drec[:, n, :].unsqueeze(2).broadcast_to([128, QUADS, 128]), ALU.mult)\
                    .then_inc(s["f_divided"], 1)

            for n in range(4 * MH):
                p_unit = p_sb[:, (n // 4) % 2, n % 4, :, :]
                pool.wait_ge(s["f_maxed"], n + 1)
                pool.tensor_tensor(p_unit, p_unit, m_sb[:, (n // 4) % 2, n % 4, :].unsqueeze(2)
                                   .broadcast_to([128, QUADS, 128]), ALU.subtract).then_inc(s["f_subbed"], 1)
                if n >= 2:
                    mha_divide(n - 2)
            mha_divide(4 * MH - 2)
            mha_divide(4 * MH - 1)
            with pool.Fori(0, B // 2) as i:
                for u in range(2):
                    pool.wait_ge(s["veps_ready"], T + 2 * i + u + 1)
                    pool.tensor_tensor(rs2[:, u:u + 1], ve2[:, u:u + 1], minus_half[:, :], ALU.pow).then_inc(s["pow_done"], 1)
            pool.wait_ge(s["crep_copied"], 1)
            pool.wait_ge(s["ffn_w_in"], 16 * nloads[0])
            pool.wait_ge(s["f_pT_done"], 4 * MH)
            pool.tensor_tensor(cblk, crep[:, :].unsqueeze(1).broadcast_to([128, B, D]),
                               batchof[:, :].unsqueeze(2).broadcast_to([128, B, D]), ALU.mult).then_inc(s["cblk_ready"], 1)
            pool.wait_ge(s["y0_ready"], B)
            pool.tensor_tensor(x_sb[:, :, :], x_sb[:, :, :], ln_rows[:, 3, :].unsqueeze(1).broadcast_to([128, B, D]),
                               ALU.add).then_inc(s["xb_ready"], 1)
            with pool.Fori(0, B // 2) as i:
                for u in range(2):
                    b = 2 * i + u
                    pool.wait_ge(s["gated"], b + 1)
                    pool.tensor_tensor(prod[:, u, 0:4, :], prod[:, u, 0:4, :], prod[:, u, 4:8, :], ALU.add)\
                        .then_inc(s["tree_step"], 1)
                    pool.wait_ge(s["tree_step"], 2 * b + 1)
                    pool.tensor_tensor(prod[:, u, 0:2, :], prod[:, u, 0:2, :], prod[:, u, 2:4, :], ALU.add)\
                        .then_inc(s["tree_step"], 1)
                    pool.wait_ge(s["tree_step"], 2 * b + 2)
                    pool.tensor_tensor(prod[:, u, 0, :], prod[:, u, 0, :], prod[:, u, 1, :], ALU.add)\
                        .then_inc(s["tree_done"], 1)
                for u in range(2):
                    pool.wait_ge(s["veps_ready"], T + B + 2 * i + u + 1)
                    pool.tensor_tensor(rs2[:, u:u + 1], ve2[:, u:u + 1], minus_half[:, :], ALU.pow).then_inc(s["pow_done"], 1)

        @block.scalar
        def _(act):
            act.wait_ge(s["ones_ready"], 5)

            def exp_unit(c, j, u):
                act.wait_ge(s["subbed"], 4 * c + j + 1)
                act.activation(p_sb[:, u, j, :, :], p_sb[:, u, j, :, :], ACT.Exp, scale=HD ** -0.5)\
                   .then_inc(s["exped"], 1)

            def pT_copy(p, j, u):
                act.wait_ge(s["pT_done"], 4 * p + j + 1)
                if j == 0 and late(p, 2):
                    act.wait_ge(s["pv_done"], p - 1)
                act.copy(pT[:, u, j, :, :], quad[4 + j % 2]).then_inc(s["pT_copied"], 1)

            def v_copy(h, u):
                act.wait_ge(s["qkv_done"], h + 1)
                if late(h, 2):
                    act.wait_ge(s["pv_done"], h - 1)
                act.copy(vaug[:, u, :, 0:HD], bank[0][:, 2 * D:3 * D].rearrange("p (h d) -> p h d", d=HD))\
                   .then_inc(s["v_copied"], 1)

            def quad_copy(h, name, dst):
                act.wait_ge(s[name + "T_done"], h + 1)
                if late(h, 2):
                    act.wait_ge(s["s_done"], 4 * h - 4)
                act.copy(dst, quad[1]).then_inc(s[name + "_copied"], 1)

            def step(t, u, layer):
                h, c, p, o = t - 1, t - 2, t - 3, t - 4
                if late(c):
                    v_copy(c, u)
                if late(h):
                    act.wait_ge(s["xT_done"], h + 1)
                    if late(h, 1):
                        act.wait_ge(s["qkv_done"], h)
                    act.copy(xnT[:, :], bank[0][:, 384:512]).then_inc(s["xnT_copied"], 1)
                if late(p):
                    exp_unit(p, 3, 1 - u)
                    pT_copy(p, 0, 1 - u)
                    pT_copy(p, 1, 1 - u)
                if late(c):
                    exp_unit(c, 0, u)
                if late(h):
                    quad_copy(h, "q4", q4[:, 1 - u, :, :])
                if late(p):
                    pT_copy(p, 2, 1 - u)
                if late(c):
                    exp_unit(c, 1, u)
                if late(h):
                    quad_copy(h, "k4", k4[:, 1 - u, :, :])
                if late(p):
                    pT_copy(p, 3, 1 - u)
                if late(c):
                    exp_unit(c, 2, u)
                if late(p):
                    act.wait_ge(s["pv_done"], p + 1)
                    if late(p, 1):
                        act.wait_ge(s["o4_done"], p)
                    act.copy(oT[:, :, :], quad[6]).then_inc(s["oT_copied"], 1)
                if late(o):
                    act.wait_ge(s["fT_done"], o + 1)
                    if late(o, 1):
                        act.wait_ge(s["proj_done"], o)
                    act.copy(ofT[:, :], bank[1][:, 0:128]).then_inc(s["fT_copied"], 1)

            pipeline(act, step)
            for i in range(2):
                act.wait_ge(s["m_done"], i + 1)
                act.copy(mexp[:, 4 * i:4 * i + 4, :], quad[2 + i]).then_inc(s["m_copied"], 1)
            act.wait_ge(s["crep_done"], 1)
            act.copy(crep[:, :], bank[4][:, 0:128]).then_inc(s["crep_copied"], 1)
            act.wait_ge(s["cm_ready"], B)
            for i in range(4):
                act.wait_ge(s["f_xT_done"], i + 1)
                act.copy(y0T.rearrange("p b s -> p (b s)").rearrange("p (g b j) -> p b g j", b=B, j=NPOS)[:, 4 * i:4 * i + 4],
                         bank[i % 2].rearrange("p (b g j) -> p b g j", b=4, j=NPOS)).then_inc(s["f_xT_copied"], 1)
            act.wait_ge(s["ffn_w_in"], 16 * nloads[0])
            for i in range(4):
                act.wait_ge(s["qk_done"], 2 * i + 1)
                act.activation(qT[:, 4 * i:4 * i + 4, :], quad[2 * (i % 2)], ACT.Identity, bias=inb_col[:, 0:1])\
                   .then_inc(s["qT_ready"], 1)
                act.wait_ge(s["v_done"], i + 1)
                act.copy(vM[:, 4 * i:4 * i + 4, :], quad[4 + i]).then_inc(s["v_ready"], 1)

            def mha_pT_copy(n):
                act.wait_ge(s["f_pT_done"], n + 1)
                if n >= 8 and n % 4 == 0:
                    act.wait_ge(s["f_pv_done"], n // 4 - 1)
                act.copy(pT[:, (n // 4) % 2, n % 4, :, :], quad[4 + n % 2]).then_inc(s["f_pT_copied"], 1)
                if n % 4 == 3:
                    i = n // 4
                    act.wait_ge(s["f_pv_done"], i + 1)
                    act.activation(aT[:, :, 4 * NPOS * i:4 * NPOS * (i + 1)].rearrange("p b (r j) -> p r b j", r=QUADS),
                                   quad[6].rearrange("p r (b j) -> p r b j", j=NPOS), ACT.Identity,
                                   bias=inb_col[:, 2:3]).then_inc(s["aT_ready"], 1)

            for n in range(4 * MH):
                p_unit = p_sb[:, (n // 4) % 2, n % 4, :, :]
                act.wait_ge(s["f_subbed"], n + 1)
                act.activation(p_unit, p_unit, ACT.Exp, scale=MHD ** -0.5).then_inc(s["f_exped"], 1)
                if n >= 4:
                    mha_pT_copy(n - 4)
            for n in range(4 * MH - 4, 4 * MH):
                mha_pT_copy(n)
            with act.Fori(0, B // 2) as i:
                for u in range(2):
                    act.wait_ge(s["y1T_done"], 2 * i + u + 1)
                    act.copy(y1T[:, 2 * i + u, :], bank[u][:, 0:128]).then_inc(s["y1T_copied"], 1)
            act.wait_ge(s["shifted"], 1)
            act.wait_ge(s["route_step"], 3)
            act.activation(lg[:, :, :], r_a[:, :, :], ACT.Exp).then_inc(s["gexp_ready"], 1)
            act.wait_ge(s["gkT_done"], 1)
            act.copy(gkT[:, :], bank[4][:, 0:128]).then_inc(s["gkT_copied"], 1)

        @block.tensor
        def _(pe):
            pe.wait_ge(s["consts_in"], 32)
            pe.wait_ge(s["ones_ready"], 5)
            pe.wait_ge(s["attn_w_in"], 32)

            def s_unit(c, j, u):
                if j == 0:
                    pe.wait_ge(s["k4_copied"], c + 1)
                if late(c, 1) or j >= 2:
                    pe.wait_ge(s["added"], 4 * c + j - 1)
                rows = slice(32 * j, 32 * j + 32)
                for r in range(QUADS):
                    mm = pe.matmul(bank[2 + j % 2][:, r * S:(r + 1) * S], q4[rows, u, r, :], k4[rows, u, r, :],
                                   start=True, stop=True)
                mm.then_inc(s["s_done"], 1)

            def pT_unit(p, j, u):
                pe.wait_ge(s["exped"], 4 * p + j + 1)
                if late(p, 1) or j >= 2:
                    pe.wait_ge(s["pT_copied"], 4 * p + j - 1)
                for r in range(QUADS):
                    mm = pe.transpose(bank[4 + j % 2][:, r * S:(r + 1) * S], p_sb[:, u, j, r, :], ident[:, :])
                mm.then_inc(s["pT_done"], 1)

            def project(h, u, layer):
                pe.wait_ge(s["xnT_copied"], h + 1)
                if layer_of(h, layer) == 0:
                    pe.matmul(bank[0][:, 0:3 * D], xnT[:, :], w_qkv_sb[:, :], start=True, stop=True)\
                      .then_inc(s["qkv_done"], 1)
                else:
                    if isinstance(h, int) and h == B:
                        pe.wait_ge(s["xw_in"], 64)
                    pe.matmul(bank[0][:, 0:D], xnT[:, :], wq_sb[:, :], start=True, stop=True)
                    pe.wait_ge(s["cm_ready"], h - B + 1)
                    for e in range(NBUCKET):
                        mm = pe.matmul(bank[0][:, D:3 * D], cm[:, u, e, :], wkv_sb[:, e, :],
                                       start=(e == 0), stop=(e == NBUCKET - 1))
                    mm.then_inc(s["qkv_done"], 1)

            def step(t, u, layer):
                h, c, p, o, f = t - 1, t - 2, t - 3, t - 4, t - 5
                if late(f):
                    pe.wait_ge(s["fT_copied"], f + 1)
                    lf = layer_of(f, layer)
                    mm = pe.matmul(bank[1][:, 128:256], ofT[:, :], w_out_sb[:, lf, :], start=True, stop=(lf == 0))
                    if lf:
                        mm = pe.matmul(bank[1][:, 128:256], ones_row[:, :], bo_row[:, :], start=False, stop=True)
                    mm.then_inc(s["proj_done"], 1)
                if late(h):
                    pe.wait_ge(s["xn_ready"], h + 1)
                    if late(h, 1):
                        pe.wait_ge(s["split_done"], 2 * h)
                        pe.wait_ge(s["v_copied"], h)
                    pe.transpose(bank[0][:, 384:512], xn[:, :], ident[:, :]).then_inc(s["xT_done"], 1)
                if late(c):
                    s_unit(c, 0, u)
                    s_unit(c, 1, u)
                if late(p):
                    pT_unit(p, 0, 1 - u)
                if late(h):
                    project(h, 1 - u, layer)
                if late(p):
                    pT_unit(p, 1, 1 - u)
                if late(c):
                    s_unit(c, 2, u)
                if late(h):
                    pe.wait_ge(s["split_done"], 2 * h + 1)
                    if late(f):
                        pe.wait_ge(s["resid_done"], f + 1)
                    for r in range(QUADS):
                        mm = pe.transpose(quad[1][:, r, :], qs[:, 4 * r:4 * r + 4, :, :, :]
                                          .rearrange("p j b a d -> p (j b a d)"), ident[:, :])
                    mm.then_inc(s["q4T_done"], 1)
                if late(p):
                    pT_unit(p, 2, 1 - u)
                if late(c):
                    s_unit(c, 3, u)
                if late(h):
                    pe.wait_ge(s["split_done"], 2 * h + 2)
                    pe.wait_ge(s["q4_copied"], h + 1)
                    for r in range(QUADS):
                        mm = pe.transpose(quad[1][:, r, :], ks[:, 4 * r:4 * r + 4, :, :, :]
                                          .rearrange("p j b a d -> p (j b a d)"), ident[:, :])
                    mm.then_inc(s["k4T_done"], 1)
                if late(p):
                    pT_unit(p, 3, 1 - u)
                if late(o):
                    pe.wait_ge(s["oT_copied"], o + 1)
                    if late(o, 1):
                        pe.wait_ge(s["o_ready"], o)
                    for r in range(QUADS):
                        mm = pe.transpose(quad[7][:, r, :], oT[:, r, :], ident[:, :])
                    mm.then_inc(s["o4_done"], 1)
                if late(p):
                    pe.wait_ge(s["pT_copied"], 4 * p + 4)
                    pe.wait_ge(s["v_copied"], p + 1)
                    if late(p, 1):
                        pe.wait_ge(s["oT_copied"], p)
                    for r in range(QUADS):
                        for j in range(QUADS):
                            mm = pe.matmul(quad[6][32 * j:32 * j + 32, r, :], vaug[:, 1 - u, 4 * r + j, :],
                                           pT[:, 1 - u, j, r, :], start=True, stop=True, skip_group_check=True)
                    mm.then_inc(s["pv_done"], 1)
                if late(o):
                    pe.wait_ge(s["o_ready"], o + 1)
                    if late(h):
                        pe.wait_ge(s["k4_copied"], h + 1)
                    pe.transpose(bank[1][:, 0:128], o_sb[:, :], ident[:, :]).then_inc(s["fT_done"], 1)

            pipeline(pe, step)
            pe.wait_ge(s["ffn_w_in"], 16 * nloads[0])
            pe.wait_ge(s["added"], 4 * T)
            for e in range(E):
                for c in range(FC):
                    mm = pe.matmul(bank[2 + e // 4][:, (e % 4) * D:(e % 4 + 1) * D], w1t_sb[:, e, c, :], w2_sb[:, e, c, :],
                                   start=(c == 0), stop=(c == FC - 1))
                if e % 4 == 3:
                    mm.then_inc(s["m_done"], 1)
            pe.wait_ge(s["pT_copied"], 4 * T)
            for e in range(E):
                for c in range(FC):
                    mm = pe.matmul(bank[4][:, e:e + 1], w2_sb[:, e, c, :], b1t_sb[:, c, e:e + 1],
                                   start=(c == 0), stop=(c == FC - 1))
            mm.then_inc(s["cT_done"], 1)
            pe.wait_ge(s["crepT_ready"], 1)
            pe.transpose(bank[4][:, 0:128], crepT[:, :, :].rearrange("p b e -> p (b e)"), ident[:, :])\
              .then_inc(s["crep_done"], 1)
            for b in range(B):
                pe.wait_ge(s["y0_ready"], b + 1)
                if b % 4 == 0 and b >= 8:
                    pe.wait_ge(s["f_xT_copied"], b // 4 - 1)
                mm = pe.transpose(quad[(b // 4) % 2][:, b % 4, :], y0[:, b, :], ident[:, :])
                if b % 4 == 3:
                    mm.then_inc(s["f_xT_done"], 1)
            pe.wait_ge(s["f_xT_copied"], 4)
            pe.wait_ge(s["m_copied"], 2)
            pe.wait_ge(s["crep_copied"], 1)
            for i in range(4):
                if i >= 2:
                    pe.wait_ge(s["qT_ready"], i - 1)
                    pe.wait_ge(s["kT_ready"], i - 1)
                for a in range(2):
                    pe.matmul(bank[2 * (i % 2) + a], inw_sb[:, a * D:(a + 1) * D], y0T[:, 4 * i:4 * i + 4, :],
                              start=True, stop=True).then_inc(s["qk_done"], 1)
                for g in range(4 * i, 4 * i + 4):
                    mm = pe.matmul(quad[4 + i][:, g % 4, :], y0T[:, g, :], inw_sb[:, 2 * D:3 * D], start=True, stop=True)
                mm.then_inc(s["v_done"], 1)
            pe.wait_ge(s["qT_ready"], 4)
            pe.wait_ge(s["kT_ready"], 4)
            pe.wait_ge(s["v_ready"], 4)

            def mha_pT_unit(n):
                pe.wait_ge(s["f_divided"], n + 1)
                if n >= 2:
                    pe.wait_ge(s["f_pT_copied"], n - 1)
                for r in range(QUADS):
                    mm = pe.transpose(quad[4 + n % 2][:, r, :], p_sb[:, (n // 4) % 2, n % 4, r, :], ident[:, :])
                mm.then_inc(s["f_pT_done"], 1)
                if n % 4 == 3:
                    i = n // 4
                    pe.wait_ge(s["f_pT_copied"], n + 1)
                    if i >= 1:
                        pe.wait_ge(s["aT_ready"], i)
                    for r in range(QUADS):
                        for j in range(MH):
                            mm = pe.matmul(quad[6][32 * j:32 * j + 32, r, :], vM[:, 4 * i + r, MHD * j:MHD * (j + 1)],
                                           pT[:, i % 2, j, r, :], start=True, stop=True, skip_group_check=True)
                    mm.then_inc(s["f_pv_done"], 1)

            for n in range(4 * MH):
                i, j = n // 4, n % 4
                if n >= 4:
                    pe.wait_ge(s["f_added"], n - 3)
                rows = slice(MHD * j, MHD * (j + 1))
                for r in range(QUADS):
                    mm = pe.matmul(quad[j][:, r, :], qT[rows, 4 * i + r, :], kT[rows, 4 * i + r, :], start=True, stop=True)
                mm.then_inc(s["f_s_done"], 1)
                if n >= 4:
                    mha_pT_unit(n - 4)
            for n in range(4 * MH - 4, 4 * MH):
                mha_pT_unit(n)
            pe.wait_ge(s["aT_ready"], 4)

            def gate_logits(b):
                if b >= 2:
                    pe.wait_ge(s["y1T_copied"], b - 1)
                pe.wait_ge(s["y1_ready"], b + 1)
                pe.transpose(bank[b % 2][:, 0:128], y1[:, b, :], ident[:, :]).then_inc(s["y1T_done"], 1)
                pe.wait_ge(s["y1T_copied"], b + 1)
                pe.matmul(bank[3][:, b * E:(b + 1) * E], y1T[:, b, :], wg_sb[:, :], start=True, stop=True)\
                  .then_inc(s["logits_done"], 1)

            for b in range(B):
                if b >= 2:
                    pe.wait_ge(s["z_ready"], b - 1)
                pe.matmul(bank[6 + b % 2][:, 0:D], aT[:, b, :], ow_sb[:, :], start=True, stop=False)
                pe.matmul(bank[6 + b % 2][:, 0:D], ones_row[:, :], ob_row[:, :], start=False, stop=True)\
                  .then_inc(s["f_proj_done"], 1)
                if b >= 1:
                    gate_logits(b - 1)
            gate_logits(B - 1)
            pe.wait_ge(s["cum_ready"], 1)
            pe.matmul(bank[2][:, 0:B * E], before[:, :], pick_bf[:, :, :].rearrange("p b e -> p (b e)"), start=True, stop=False)
            pe.matmul(bank[2][:, 0:B * E], ones_bf[:, :], cum_bf[:, :, :].rearrange("p b e -> p (b e)"), start=False, stop=True)\
              .then_inc(s["place_done"], 1)
            pe.wait_ge(s["gk_ready"], 1)
            pe.transpose(bank[4][:, 0:128], gk[:, :, :].rearrange("p b e -> p (b e)"), ident[:, :]).then_inc(s["gkT_done"], 1)
            for b in range(B):
                u = b % 2
                if b >= 2:
                    pe.wait_ge(s["gated"], b - 1)
                for a in range(2):
                    mm = pe.matmul(bank[2 * u + a], y1T[:, b, :], mexp[:, 4 * a:4 * a + 4, :], start=True, stop=True)
                mm.then_inc(s["ffn_done"], 1)
                if b == 0:
                    pe.wait_ge(s["gkT_copied"], 1)
                    pe.wait_ge(s["cblk_ready"], 1)
                if b >= 2:
                    pe.wait_ge(s["z_ready"], B + 2 * (b - 2) + 1)
                pe.matmul(bank[6 + u][:, 0:D], gkT[:, :], cblk[:, b, :], start=True, stop=True).then_inc(s["bias_done"], 1)




def kernel(**inputs):
    import numpy as _np
    import concourse.bacc as _bacc
    from concourse import mybir as _mybir
    from concourse.bass_utils import run_bass_kernel_spmd as _run

    a = {k: _np.asarray(v) for k, v in inputs.items()}
    import ml_dtypes
    bf = ml_dtypes.bfloat16
    p = _np.arange(128)
    arrays = {
        "x": a["x"],
        "ctxT": a["ctx_1024"].transpose(0, 2, 1),
        "fside": a["fside_BxS2_0"],
        "fsideT": a["fside_BxS2_0"].T,
        "itok": a["itok_BxS2_0_7"],
        "pad": a["mask_BxS2_bf0"].view(_np.int32),
        "w_qkv": a["L0_attn_w_qkv"],
        "w_out": a["L0_attn_w_out"],
        "wq": a["L0_xattn_Wq"],
        "wkv": _np.concatenate([a["L0_xattn_Wk_b"], a["L0_xattn_Wv_b"]], axis=2),
        "wo": a["L0_xattn_Wo"],
        "bo": a["L0_xattn_bo"][None],
        "inw": a["L0_ffn_in_proj_w"].T,
        "inb": a["L0_ffn_in_proj_b"].reshape(3, D).T,
        "ow": a["L0_ffn_out_proj_w"].T,
        "ob": a["L0_ffn_out_proj_b"][None],
        "g1": a["L0_ffn_ln1_g"],
        "be1": a["L0_ffn_ln1_b"],
        "g2": a["L0_ffn_ln2_g"],
        "be2": a["L0_ffn_ln2_b"],
        "wg": a["L0_ffn_wg"],
        "w1t": a["L0_ffn_w1"].transpose(0, 2, 1),
        "b1t": a["L0_ffn_b1"].T,
        "w2": a["L0_ffn_w2"],
        "b2t": a["L0_ffn_b2"].T,
        "c_ident": _np.eye(128, dtype=_np.float32),
        "c_causal": _np.where(p[:, None] >= p[None, :], 0.0, NEG).astype(_np.float32),
        "c_samepos": _np.where(p[:, None] % 8 == p[None, :] % 8, 0.0, NEG).astype(_np.float32),
        "c_before": (p[:, None] < p[None, :]).astype(bf),
        "c_rank": _np.broadcast_to(_np.arange(E, 0, -1, dtype=_np.float32), (128, B, E)),
        "c_batchof": (p[:, None] // E == _np.arange(B)[None, :]).astype(_np.float32),
    }
    arrays = {k: _np.ascontiguousarray(v) for k, v in arrays.items()}
    nc = _bacc.Bacc("TRN2", target_bir_lowering=False, num_devices=1)
    args = {k: nc.dram_tensor(k, v.shape, _mybir.dt.from_np(v.dtype), kind="ExternalInput").ap()
            for k, v in arrays.items()}
    out = nc.dram_tensor("out", (B, S, D), _mybir.dt.float32, kind="ExternalOutput").ap()
    decoder_kernel(nc, **args, out=out)
    r = _run(nc, [arrays], core_ids=[0])
    return r.results[0]["out"]
```

```python
import numpy as np
import concourse.bass as bass
from concourse import mybir
from contextlib import ExitStack

B, S, D = 16, 128, 128
H, HD = 16, 8
NBUCKET = 8
MH, MHD = 4, 32
E, FF = 8, 512
CAP = B * S // E
EPS = 1e-5
MASKED = float(2 ** 100)
QUADS = 4
LAGS = 4
PEEL = 6


def decoder_kernel(nc, x, ctxT, fside, fsideT, itok, pad, w_qkv, w_out, wq, wkv, wo, bo,
                   inw, inb, ow, ob, g1, be1, g2, be2, wg, w1t, b1t, w2, b2t,
                   c_ident, c_ident_bf, c_causal, c_samepos, c_before, c_rank, c_batchof, out):
    f32, f32r, bf16 = mybir.dt.float32, mybir.dt.float32r, mybir.dt.bfloat16
    ALU, ACT, AX = mybir.AluOpType, mybir.ActivationFunctionType, mybir.AxisListType
    FC = FF // 128
    T = 2 * B
    nloads = [0]
    NPOS = S // B

    st = ExitStack()
    with st:
        def sb(name, shape, dt=f32):
            return st.enter_context(nc.sbuf_tensor(name, shape, dt))

        def sem(name):
            return st.enter_context(nc.semaphore(name))

        w_qkv_sb = sb("w_qkv_sb", [128, 3 * D])
        w_out_sb = sb("w_out_sb", [128, 2, D])
        wq_sb = sb("wq_sb", [128, D])
        wkv_sb = sb("wkv_sb", [128, NBUCKET, 2 * D])
        bo_row = sb("bo_row", [1, D])
        ones_row = sb("ones_row", [1, 128])
        inw_sb = sb("inw_sb", [128, 3 * D])
        inb_col = sb("inb_col", [128, 3])
        ow_sb = sb("ow_sb", [128, D])
        ob_row = sb("ob_row", [1, D])
        ln_rows = sb("ln_rows", [128, 4, D])
        wg_sb = sb("wg_sb", [128, E])
        w1t_sb = sb("w1t_sb", [128, E, FC, D])
        w2_sb = sb("w2_sb", [128, E, FC, D])
        b1t_sb = sb("b1t_sb", [128, FC, E])
        b2t_sb = sb("b2t_sb", [128, E])
        ident = sb("ident", [128, 128])
        causal = sb("causal", [128, 128], bf16)
        ident_bf = sb("ident_bf", [128, 128], bf16)
        samepos = sb("samepos", [128, 128], bf16)
        before = sb("before", [128, 128], bf16)
        ones_bf = sb("ones_bf", [128, 128], bf16)
        rank = sb("rank", [128, B, E])
        batchof = sb("batchof", [128, B])
        x_sb = sb("x_sb", [128, B, D])
        ctx_sb = sb("ctx_sb", [128, B, S])
        itok_i = sb("itok_i", [128, B, S], mybir.dt.int32)
        itok_bf = sb("itok_bf", [128, B, S], bf16)
        onehot = sb("onehot", [128, NBUCKET, B, S], bf16)
        tk = sb("tk", [128, B, S])
        tq = sb("tq", [128, B])
        pad_words = sb("pad_words", [128, B, S // 4], mybir.dt.int32)
        pad_big = sb("pad_big", [128, B, S])
        xmask = pad_big[:, :, :].rearrange("p b s -> p (b s)").bitcast(bf16)[:, 0:B * S]\
            .rearrange("p (b s) -> p b s", b=B)

        stats = sb("stats", [128, 6])
        mv = sb("mv", [128, 2])
        veps = sb("veps", [128, 1])
        minus_half = sb("minus_half", [128, 1])
        rstd = sb("rstd", [128, 1])
        xn = sb("xn", [128, D])
        xnT = sb("xnT", [128, S])
        cm = sb("cm", [128, NBUCKET, S])
        kv_sb = sb("kv_sb", [128, B, 2, D])
        qs = sb("qs", [128, H, 2, 2, HD])
        ks = sb("ks", [128, H, 2, 2, HD])
        q4 = sb("q4", [128, 2, QUADS, S], f32r)
        k4 = sb("k4", [128, 2, QUADS, S], f32r)
        v_sb = sb("v_sb", [128, D])
        vaug = sb("vaug", [128, 2, H, 32])
        p_sb = sb("p_sb", [128, 2, QUADS, QUADS, S])
        m_sb = sb("m_sb", [128, 2, QUADS, QUADS])
        pT = sb("pT", [128, 2, QUADS, QUADS, S])
        oT = sb("oT", [128, QUADS, S])
        rden = sb("rden", [128, QUADS, QUADS])
        o_sb = sb("o_sb", [128, D])
        ofT = sb("ofT", [128, S])


        free = onehot[:, :, :, :].rearrange("p e b s -> p (e b s)").bitcast(f32)
        spans = [free[:, i * B * S:(i + 1) * B * S].rearrange("p (b s) -> p b s", b=B) for i in range(4)]
        y0T, qT, z16, aT = spans
        y0 = itok_i[:, :, :].bitcast(f32)
        y1 = tk[:, :, :]
        y1T = pad_big[:, :, :]
        vM = ctx_sb[:, :, :]
        prod = pT[:, :, :, :, :].rearrange("p u j r q -> p u (j r q)")[:, :, 0:E * D]\
            .rearrange("p u (e d) -> p u e d", e=E)
        mexp = cm[:, :, :]
        cT = sb("cT", [128, E])
        cblk = p_sb[:, 0, :, :, :].rearrange("p j r k -> p (j r) k")
        crepT = sb("crepT", [128, B, E])
        crep = sb("crep", [128, D])
        st16 = sb("st16", [128, B, 6])
        mv16 = sb("mv16", [128, B, 2])
        ve16 = sb("ve16", [128, B])
        half16 = sb("half16", [128, B])
        rs16 = sb("rs16", [128, B])
        spare = kv_sb[:, :, :, :].rearrange("p b a d -> p (b a d)")
        used = [0]

        def over_kv(n, *dims):
            used[0] += n
            part = spare[:, used[0] - n:used[0]]
            return part.rearrange("p (a b) -> p a b", b=dims[0]) if dims else part

        dsum = over_kv(4 * MH * QUADS, QUADS)
        drec = over_kv(4 * MH * QUADS, QUADS)
        lg, r_a, r_b = (over_kv(B * E, E) for _ in range(3))
        r_m, r_s = over_kv(B), over_kv(B)
        gate = over_kv(B)
        kept = over_kv(B * E, E)
        keptT = over_kv(128)
        keptT_bf = sb("keptT_bf", [128, 128], bf16)
        pick_bf = sb("pick_bf", [128, B, E], bf16)

        def kblk(rows, g, n):
            half = (w1t_sb, w2_sb)[g // 8][rows, :, :, :].rearrange("p e c d -> p (e c d)")\
                .rearrange("p (g j s) -> p g j s", g=B // 2, j=MH)
            return half[:, g % 8:g % 8 + n]

        ps = st.enter_context(nc.psum_tensor("ps", [128, 8, 512], f32))
        bank = [ps[:, i, :] for i in range(8)]
        quad = [b.rearrange("p (r k) -> p r k", r=QUADS) for b in bank]

        names = """consts_in x_in x_rest_in wqkv_in attn_w_in ctx_in xw_in ffn_w_in ones_ready bn_step veps_ready
            pow_done xn_ready xT_done xnT_copied qkv_done hi_done split_done v_copied v_placed q4T_done q4_copied
            k4T_done k4_copied s_done least_ready exped wq_ready w_ffq_ready pT_done pT_copied pv_done oT_copied
            o4_done den_done o_ready fT_done fT_copied proj_done resid_done onehot_step mask_step cm_ready kv_done
            kv_copied stored m_done m_copied cT_done cT_ready crepT_ready crep_done crep_copied st_step mv_step
            ve_ready rs_ready y0_ready f_xT_done f_xT_copied qk_done qT_ready kblk_zeroed k_ready k_last_ready
            v_done v_ready f_s_done f_least_ready f_exped f_sum f_drec f_divided f_pT_done f_pT_copied f_pv_done
            aT_ready f_proj_done z_ready w_ready wg_step y1_ready y1T_done y1T_copied logits_done route_step
            shifted gexp_ready pick_ready gate_ready place_done kept_ready keptT_done keptT_copied cblk_ready
            xb_ready hot_done gated ffn_done out_rows""".split()
        assert len(names) == len(set(names))
        s = {n: sem(n) for n in names}
        block = st.enter_context(nc.Block())

        def late(k, n=0):
            return not isinstance(k, int) or n <= k < T

        def layer_of(k, layer):
            return layer if not isinstance(k, int) else int(k >= B)

        def batch(k, layer):
            return k - B if layer_of(k, layer) else k

        def pipeline(e, step):
            for layer in range(2):
                for t in range(layer * B, layer * B + PEEL):
                    step(t, t % 2, layer, t // 2)
                with e.Fori((layer * B + PEEL) // 2, (layer + 1) * B // 2) as i:
                    step(2 * i, 0, layer, i)
                    step(2 * i + 1, 1, layer, i)
            for t in range(T, T + LAGS):
                step(t, t % 2, 1, t // 2)

        def bcast(v):
            return v.unsqueeze(2).broadcast_to([128, B, E])


        @block.sync
        def _(sp):
            sp.dma_start(x_sb[:, 0:4, :], x[0:4].rearrange("b s d -> s b d")).then_inc(s["x_in"], 16)
            sp.dma_start(ident[:, :], c_ident).then_inc(s["consts_in"], 16)
            sp.dma_start(w_qkv_sb[:, :], w_qkv).then_inc(s["wqkv_in"], 16)
            sp.dma_start(causal[:, :], c_causal).then_inc(s["consts_in"], 16)
            sp.dma_start(ident_bf[:, :], c_ident_bf).then_inc(s["consts_in"], 16)
            sp.dma_start(x_sb[:, 4:B, :], x[4:B].rearrange("b s d -> s b d")).then_inc(s["x_rest_in"], 16)
            sp.dma_start(w_out_sb[:, 0, :], w_out).then_inc(s["attn_w_in"], 16)
            sp.dma_start(itok_i[:, :, :], itok.partition_broadcast(128)).then_inc(s["ctx_in"], 16)
            sp.dma_start(pad_words[:, :, :], pad.partition_broadcast(128)).then_inc(s["ctx_in"], 16)
            sp.dma_start(ctx_sb[:, :, :], ctxT.rearrange("b d s -> d b s")).then_inc(s["ctx_in"], 16)
            sp.dma_start(tk[:, :, :], fside.partition_broadcast(128)).then_inc(s["ctx_in"], 16)
            sp.dma_start(tq[:, :], fsideT).then_inc(s["ctx_in"], 16)
            sp.dma_start(wq_sb[:, :], wq).then_inc(s["xw_in"], 16)
            sp.dma_start(wkv_sb[:, :, :], wkv.rearrange("e d n -> d e n")).then_inc(s["xw_in"], 16)
            sp.dma_start(w_out_sb[:, 1, :], wo).then_inc(s["xw_in"], 16)
            sp.dma_start(bo_row[:, :], bo).then_inc(s["xw_in"], 16)
            loads = [(w1t_sb[:, :, :, :], w1t.rearrange("e (c p) d -> p e c d", p=128)),
                     (w2_sb[:, :, :, :], w2.rearrange("e (c p) d -> p e c d", p=128)),
                     (b1t_sb[:, :, :], b1t.rearrange("(c p) e -> p c e", p=128)), (b2t_sb[:, :], b2t),
                     (inw_sb[:, :], inw), (inb_col[:, :], inb), (ow_sb[:, :], ow), (ob_row[:, :], ob),
                     (wg_sb[:, :], wg), (samepos[:, :], c_samepos), (before[:, :], c_before),
                     (rank[:, :, :], c_rank), (batchof[:, :], c_batchof)]
            loads += [(ln_rows[:, i, :], v.partition_broadcast(128)) for i, v in enumerate((g1, be1, g2, be2))]
            for dst, src in loads:
                sp.dma_start(dst, src).then_inc(s["ffn_w_in"], 16)
            nloads[0] = len(loads)
            for i in range(B // 2):
                sp.wait_ge(s["out_rows"], 2 * i + 2)
                sp.dma_start(out[2 * i:2 * i + 2].rearrange("b s d -> s b d"), y0[:, 2 * i:2 * i + 2, :]).then_inc(s["stored"], 16)
            sp.wait_ge(s["stored"], 16 * (B // 2))

        @block.vector
        def _(dve):
            dve.memset(ones_row[:, :], 1.0).then_inc(s["ones_ready"], 1)
            dve.memset(vaug[:, :, :, :], 1.0).then_inc(s["ones_ready"], 1)
            dve.memset(minus_half[:, :], -0.5).then_inc(s["ones_ready"], 1)
            dve.memset(half16[:, :], -0.5).then_inc(s["ones_ready"], 1)
            dve.memset(ones_bf[:, :], 1.0).then_inc(s["ones_ready"], 1)
            dve.wait_ge(s["wqkv_in"], 16)
            dve.tensor_scalar(w_qkv_sb[:, 0:D], w_qkv_sb[:, 0:D], -HD ** -0.5, None, ALU.mult)\
               .then_inc(s["wq_ready"], 1)
            dve.wait_ge(s["x_in"], 16)

            def norm_stats(t, layer):
                dve.bn_stats(stats[:, :], x_sb[:, batch(t, layer), :]).then_inc(s["bn_step"], 1)

            def norm_variance(t):
                if isinstance(t, int):
                    dve.wait_ge(s["bn_step"], 2 * t + 1)
                    if t >= 1:
                        dve.wait_ge(s["xn_ready"], t)
                dve.bn_aggr(mv[:, :], stats[:, :]).then_inc(s["bn_step"], 1)
                dve.wait_ge(s["bn_step"], 2 * t + 2)
                if late(t, 1):
                    dve.wait_ge(s["pow_done"], t)
                dve.tensor_scalar(veps[:, :], mv[:, 1:2], EPS, None, ALU.add).then_inc(s["veps_ready"], 1)

            def norm_rows(t, layer):
                dve.wait_ge(s["pow_done"], t + 1)
                if late(t, 1):
                    dve.wait_ge(s["xT_done"], t)
                dve.tensor_scalar(xn[:, :], x_sb[:, batch(t, layer), :], mv[:, 0:1], rstd[:, :],
                                  ALU.subtract, ALU.mult).then_inc(s["xn_ready"], 1)

            def split(h, layer):
                dve.wait_ge(s["qkv_done"], h + 1)
                q, k = bank[0][:, 0:D], bank[0][:, D:2 * D]
                if layer_of(h, layer):
                    dve.wait_ge(s["kv_copied"], 2 * (h - B) + 1)
                    k = kv_sb[:, h - B, 0, :]
                q, k = (a.rearrange("p (h d) -> p h d", d=HD).unsqueeze(2).broadcast_to([128, H, 2, HD])
                        for a in (q, k))
                if late(h, 1):
                    dve.wait_ge(s["k4T_done"], h)
                dve.tensor_copy(qs[:, :, :, 0, :].bitcast(f32r), q).then_inc(s["hi_done"], 1)
                dve.tensor_copy(ks[:, :, 0, :, :].bitcast(f32r), k).then_inc(s["hi_done"], 1)
                dve.wait_ge(s["hi_done"], 2 * h + 1)
                dve.tensor_tensor(qs[:, :, :, 1, :], q, qs[:, :, :, 0, :], ALU.subtract).then_inc(s["split_done"], 1)
                dve.wait_ge(s["hi_done"], 2 * h + 2)
                dve.tensor_tensor(ks[:, :, 1, :, :], k, ks[:, :, 0, :, :], ALU.subtract).then_inc(s["split_done"], 1)

            def unit(c, j, u):
                dve.wait_ge(s["s_done"], 4 * c + j + 1)
                if j == 0 and late(c, 2):
                    dve.wait_ge(s["exped"], 4 * c - 4)
                dve.tensor_reduce(m_sb[:, u, j, :], quad[2 + j % 2], AX.X, ALU.min).then_inc(s["least_ready"], 1)

            def k4_copy(h, u):
                dve.wait_ge(s["k4T_done"], h + 1)
                if late(h, 2):
                    dve.wait_ge(s["s_done"], 4 * h - 4)
                dve.tensor_copy(k4[:, u, :, :], quad[1]).then_inc(s["k4_copied"], 1)

            def divide(o):
                dve.wait_ge(s["o4_done"], o + 1)
                o4 = bank[7].rearrange("p (r j c) -> p r j c", r=QUADS, j=QUADS)
                dve.reciprocal(rden[:, :, :], o4[:, :, :, HD]).then_inc(s["den_done"], 1)
                dve.wait_ge(s["den_done"], o + 1)
                if late(o, 1):
                    dve.wait_ge(s["fT_done"], o)
                dve.tensor_tensor(o_sb[:, :].rearrange("p (r j c) -> p r j c", r=QUADS, j=QUADS),
                                  o4[:, :, :, 0:HD],
                                  rden[:, :, :].unsqueeze(3).broadcast_to([128, QUADS, QUADS, HD]),
                                  ALU.mult).then_inc(s["o_ready"], 1)

            def residual(f, layer):
                dve.wait_ge(s["proj_done"], f + 1)
                rows = x_sb[:, batch(f, layer), :]
                dve.tensor_tensor(rows, rows, bank[6][:, 0:D], ALU.add).then_inc(s["resid_done"], 1)

            def step(t, u, layer, pair):
                h, c, o = t - 1, t - 2, t - 4
                if isinstance(t, int) and t == 4:
                    dve.wait_ge(s["x_rest_in"], 16)
                if isinstance(t, int) and t == B:
                    dve.wait_ge(s["xw_in"], 64)
                    dve.tensor_scalar(wq_sb[:, :], wq_sb[:, :], -HD ** -0.5, None, ALU.mult)\
                       .then_inc(s["wq_ready"], 1)
                if late(t):
                    norm_stats(t, layer)
                if late(c):
                    unit(c, 0, u)
                if late(o):
                    divide(o)
                if late(t):
                    norm_variance(t)
                if late(c):
                    unit(c, 1, u)
                if late(h):
                    split(h, layer)
                if late(t):
                    norm_rows(t, layer)
                if late(c):
                    unit(c, 2, u)
                if late(o):
                    residual(o, layer)
                if late(h):
                    k4_copy(h, 1 - u)
                if late(c):
                    unit(c, 3, u)
                if isinstance(t, int) and t == 0:
                    dve.wait_ge(s["ctx_in"], 16 * 5)
                    dve.tensor_copy(itok_bf[:, :, :], itok_i[:, :, :]).then_inc(s["onehot_step"], 1)
                    dve.tensor_scalar(pad_big[:, :, :], pad_words[:, :, :].bitcast(mybir.dt.uint8), -MASKED, None,
                                      ALU.mult).then_inc(s["onehot_step"], 1)
                    dve.wait_ge(s["onehot_step"], 1)
                    for e in range(NBUCKET):
                        dve.tensor_scalar(onehot[:, e, :, :], itok_bf[:, :, :], float(e), None, ALU.is_equal)\
                           .then_inc(s["onehot_step"], 1)

                if isinstance(t, int) and t == T:
                    y0_variance(0, B - 4)
                if isinstance(t, int) and t > T:
                    y0_rows(t - T - 1)

            def y0_variance(b0, b1):
                dve.wait_ge(s["resid_done"], B + b1)
                for b in range(b0, b1):
                    dve.bn_stats(st16[:, b, :], x_sb[:, b, :]).then_inc(s["st_step"], 1)
                dve.wait_ge(s["st_step"], b1)
                for b in range(b0, b1):
                    dve.bn_aggr(mv16[:, b, :], st16[:, b, :]).then_inc(s["mv_step"], 1)
                dve.wait_ge(s["mv_step"], b1)
                dve.tensor_scalar(ve16[:, b0:b1], mv16[:, b0:b1, 1], EPS, None, ALU.add).then_inc(s["ve_ready"], 1)

            def y0_rows(i):
                dve.wait_ge(s["rs_ready"], 2 if i == 3 else 1)
                for b in range(4 * i, 4 * i + 4):
                    dve.tensor_scalar(y0[:, b, :], x_sb[:, b, :], mv16[:, b, 0:1], rs16[:, b:b + 1],
                                      ALU.subtract, ALU.mult).then_inc(s["y0_ready"], 1)

            pipeline(dve, step)
            y0_variance(B - 4, B)
            y0_rows(3)
            dve.wait_ge(s["ffn_w_in"], 16 * nloads[0])
            dve.tensor_scalar(inw_sb[:, 0:D], inw_sb[:, 0:D], -MHD ** -0.5, None, ALU.mult).then_inc(s["w_ffq_ready"], 1)
            dve.tensor_scalar(inb_col[:, 0:1], inb_col[:, 0:1], -MHD ** -0.5, None, ALU.mult).then_inc(s["w_ffq_ready"], 1)
            dve.wait_ge(s["cT_done"], 1)
            dve.tensor_tensor(cT[:, :], bank[4][:, 0:E], b2t_sb[:, :], ALU.add).then_inc(s["cT_ready"], 1)
            dve.wait_ge(s["cT_ready"], 1)
            dve.tensor_copy(crepT[:, :, :], cT[:, :].unsqueeze(1).broadcast_to([128, B, E])).then_inc(s["crepT_ready"], 1)
            for i in range(4):
                dve.wait_ge(s["qk_done"], 2 * i + 2)
                if i % 2 == 0:
                    dve.wait_ge(s["kblk_zeroed"], i // 2 + 1)
                for j in range(MH - 1):
                    rows = slice(MHD * j, MHD * (j + 1))
                    dve.tensor_scalar(kblk(rows, 4 * i, 4)[:, :, j, :], quad[2 * (i % 2) + 1][rows], inb_col[rows, 1:2], None,
                                      ALU.add).then_inc(s["k_ready"], 1)

            def mha_sum(n):
                dve.wait_ge(s["f_exped"], n + 1)
                dve.tensor_reduce(dsum[:, n, :], p_sb[:, (n // 4) % 2, n % 4, :, :], AX.X, ALU.add).then_inc(s["f_sum"], 1)
                dve.wait_ge(s["f_sum"], n + 1)
                dve.reciprocal(drec[:, n, :], dsum[:, n, :]).then_inc(s["f_drec"], 1)

            for n in range(B):
                dve.wait_ge(s["f_s_done"], n + 1)
                dve.tensor_reduce(m_sb[:, (n // 4) % 2, n % 4, :], quad[n % 4], AX.X, ALU.min).then_inc(s["f_least_ready"], 1)
                if n >= 1:
                    mha_sum(n - 1)
            mha_sum(B - 1)

            def z_stats(b, k):
                dve.wait_ge(s["z_ready"], B * k + b + 1)
                dve.bn_stats(st16[:, b, :], z16[:, b, :]).then_inc(s["st_step"], 1)

            def pair_variance(b, k):
                dve.wait_ge(s["st_step"], B * (k + 1) + b + 1)
                for a in (b - 1, b):
                    dve.bn_aggr(mv16[:, a, :], st16[:, a, :]).then_inc(s["mv_step"], 1)
                dve.wait_ge(s["mv_step"], B * (k + 1) + b + 1)
                dve.tensor_scalar(ve16[:, b - 1:b + 1], mv16[:, b - 1:b + 1, 1], EPS, None, ALU.add).then_inc(s["ve_ready"], 1)

            def z_rows(b, k):
                dve.wait_ge(s["rs_ready"], 2 + k * (B // 2) + b // 2 + 1)
                dve.tensor_scalar(z16[:, b, :], z16[:, b, :], mv16[:, b, 0:1], rs16[:, b:b + 1], ALU.subtract, ALU.mult)\
                   .then_inc(s["w_ready"], 1)

            for b in range(B + 4):
                if b < B:
                    dve.wait_ge(s["f_proj_done"], b + 1)
                    dve.tensor_tensor(z16[:, b, :], y0[:, b, :], bank[b % 4][:, 0:D], ALU.add).then_inc(s["z_ready"], 1)
                if b >= 4:
                    z_rows(b - 4, 0)
                if b < B:
                    z_stats(b, 0)
                    if b % 2:
                        pair_variance(b, 0)

            routed = [0]

            def route(ins):
                routed[0] += 1
                ins.then_inc(s["route_step"], 1)
                dve.wait_ge(s["route_step"], routed[0])

            logits = bank[6][:, 0:B * E].rearrange("p (b e) -> p b e", e=E)
            dve.wait_ge(s["logits_done"], B)
            route(dve.tensor_reduce(r_m[:, :], logits, AX.X, ALU.max))
            dve.tensor_tensor(r_a[:, :, :], logits, bcast(r_m), ALU.subtract).then_inc(s["shifted"], 1)
            route(dve.tensor_tensor(r_b[:, :, :], logits, bcast(r_m), ALU.is_equal))
            route(dve.tensor_tensor(r_b[:, :, :], r_b[:, :, :], rank[:, :, :], ALU.mult))
            route(dve.tensor_reduce(r_m[:, :], r_b[:, :, :], AX.X, ALU.max))
            dve.tensor_tensor(pick_bf[:, :, :], r_b[:, :, :], bcast(r_m), ALU.is_equal).then_inc(s["pick_ready"], 1)
            dve.wait_ge(s["gexp_ready"], 1)
            route(dve.tensor_reduce(r_s[:, :], lg[:, :, :], AX.X, ALU.add))
            dve.reciprocal(gate[:, :], r_s[:, :]).then_inc(s["gate_ready"], 1)
            dve.wait_ge(s["place_done"], 1)
            route(dve.tensor_scalar(r_b[:, :, :], bank[7][:, 0:B * E].rearrange("p (b e) -> p b e", e=E), float(CAP), None,
                                    ALU.is_lt))
            dve.tensor_tensor(kept[:, :, :], r_b[:, :, :], pick_bf[:, :, :], ALU.mult).then_inc(s["kept_ready"], 1)
            dve.wait_ge(s["gate_ready"], 1)
            for m in range(B + 5):
                if m < B:
                    dve.wait_ge(s["hot_done"], m + 1)
                    if m >= 2:
                        dve.wait_ge(s["ffn_done"], m - 1)
                    dve.tensor_tensor(prod[:, m % 2, :, :], ps[:, 2 * (m % 2):2 * (m % 2) + 2, :]
                                      .rearrange("p a (e d) -> p (a e) d", d=D),
                                      y1T[:, m, :].unsqueeze(1).broadcast_to([128, E, D]), ALU.mult).then_inc(s["gated"], 1)
                b = m - 2
                if 0 <= b < B:
                    dve.wait_ge(s["ffn_done"], b + 1)
                    dve.scalar_tensor_tensor(z16[:, b, :], bank[4 + b % 4][:, 0:D], gate[:, b:b + 1], y1[:, b, :],
                                             ALU.mult, ALU.add).then_inc(s["z_ready"], 1)
                if m >= 5:
                    z_rows(m - 5, 1)
                if 0 <= b < B:
                    z_stats(b, 1)
                    if b % 2:
                        pair_variance(b, 1)

        @block.gpsimd
        def _(pool):
            pool.wait_ge(s["ones_ready"], 5)

            def mask_part(part):
                if part == 0:
                    pool.wait_ge(s["ctx_in"], 16 * 5)
                    ins = pool.tensor_tensor(tk[:, :, :], tk[:, :, :],
                                             tq[:, :].unsqueeze(2).broadcast_to([128, B, S]), ALU.subtract)
                else:
                    pool.wait_ge(s["mask_step"], part)
                if part == 1:
                    ins = pool.tensor_scalar(tk[:, :, :], tk[:, :, :], 0.0, -MASKED, ALU.is_gt, ALU.mult)
                if part == 2:
                    pool.wait_ge(s["onehot_step"], 2)
                    ins = pool.tensor_tensor(tk[:, :, :], tk[:, :, :], pad_big[:, :, :], ALU.add)
                if part == 3:
                    ins = pool.tensor_scalar(xmask, tk[:, :, :], MASKED, 0.0, ALU.add, ALU.max)
                ins.then_inc(s["mask_step"], 1)

            def v_place_waits(c, layer):
                if layer_of(c, layer):
                    pool.wait_ge(s["kv_copied"], 2 * (c - B) + 2)
                else:
                    pool.wait_ge(s["v_copied"], c + 1)
                if late(c, 2):
                    pool.wait_ge(s["pv_done"], c - 1)

            def v_place(c, u, layer):
                v = kv_sb[:, c - B, 1, :] if layer_of(c, layer) else v_sb[:, :]
                pool.tensor_copy(vaug[:, u, :, 0:HD], v.rearrange("p (h d) -> p h d", d=HD))\
                    .then_inc(s["v_placed"], 1)

            def bucket_ctx(pair):
                if not isinstance(pair, int) or pair >= 1:
                    pool.wait_ge(s["kv_done"], 2 * pair)
                pool.tensor_tensor(cm[:, :, :], onehot[:, :, pair, :],
                                   ctx_sb[:, pair, :].unsqueeze(1).broadcast_to([128, NBUCKET, S]),
                                   ALU.mult).then_inc(s["cm_ready"], 1)

            def step(t, u, layer, pair):
                if late(t - 2):
                    v_place_waits(t - 2, layer)
                if late(t):
                    pool.wait_ge(s["veps_ready"], t + 1)
                    if late(t, 1):
                        pool.wait_ge(s["xn_ready"], t)
                    pool.tensor_tensor(rstd[:, :], veps[:, :], minus_half[:, :], ALU.pow)\
                        .then_inc(s["pow_done"], 1)
                if late(t - 2):
                    v_place(t - 2, u, layer)
                if isinstance(t, int) and 2 <= t < 6:
                    mask_part(t - 2)
                if u == 0 and late(t):
                    if isinstance(t, int) and t == 0:
                        pool.wait_ge(s["ctx_in"], 16 * 5)
                        pool.wait_ge(s["onehot_step"], NBUCKET + 2)
                    bucket_ctx(pair)

                if isinstance(t, int) and t == T:
                    y0_power(0, B - 4, 1)

            def y0_power(b0, b1, n):
                pool.wait_ge(s["ve_ready"], n)
                pool.tensor_tensor(rs16[:, b0:b1], ve16[:, b0:b1], half16[:, b0:b1], ALU.pow)\
                    .then_inc(s["rs_ready"], 1)

            pipeline(pool, step)
            y0_power(B - 4, B, 2)
            pool.wait_ge(s["m_done"], 2)
            pool.memset(w1t_sb[:, :, :, :], 0.0).then_inc(s["kblk_zeroed"], 1)
            pool.wait_ge(s["cT_done"], 1)
            pool.memset(w2_sb[:, :, :, :], 0.0).then_inc(s["kblk_zeroed"], 1)
            pool.wait_ge(s["ffn_w_in"], 16 * nloads[0])
            pool.wait_ge(s["y0_ready"], B)
            pool.tensor_tensor(x_sb[:, :, :], x_sb[:, :, :], ln_rows[:, 3, :].unsqueeze(1).broadcast_to([128, B, D]),
                               ALU.add).then_inc(s["xb_ready"], 1)
            for n in range(B):
                p_unit = p_sb[:, (n // 4) % 2, n % 4, :, :]
                pool.wait_ge(s["f_drec"], n + 1)
                pool.tensor_tensor(p_unit, p_unit, drec[:, n, :].unsqueeze(2).broadcast_to([128, QUADS, 128]), ALU.mult)\
                    .then_inc(s["f_divided"], 1)

            def norm_pairs(k, scale, bias, dst, done):
                for i in range(B // 2 + 1):
                    if i < B // 2:
                        pool.wait_ge(s["ve_ready"], 2 + k * (B // 2) + i + 1)
                        pool.tensor_tensor(rs16[:, 2 * i:2 * i + 2], ve16[:, 2 * i:2 * i + 2], half16[:, 0:2], ALU.pow)\
                            .then_inc(s["rs_ready"], 1)
                    if i >= 1:
                        pair = (2 * i - 2, 2 * i - 1)
                        for b in pair:
                            pool.wait_ge(s["w_ready"], B * k + b + 1)
                            pool.tensor_tensor(z16[:, b, :], z16[:, b, :], scale, ALU.mult).then_inc(s["wg_step"], 1)
                        for b in pair:
                            pool.wait_ge(s["wg_step"], B * k + b + 1)
                            pool.tensor_tensor(dst[:, b, :], z16[:, b, :], bias(b), ALU.add).then_inc(s[done], 1)

            norm_pairs(0, ln_rows[:, 0, :], lambda b: ln_rows[:, 1, :], y1, "y1_ready")
            pool.wait_ge(s["crep_copied"], 1)
            pool.wait_ge(s["f_pT_done"], B)
            pool.tensor_tensor(cblk, crep[:, :].unsqueeze(1).broadcast_to([128, B, D]),
                               batchof[:, :].unsqueeze(2).broadcast_to([128, B, D]), ALU.mult).then_inc(s["cblk_ready"], 1)
            pool.wait_ge(s["xb_ready"], 1)
            norm_pairs(1, ln_rows[:, 2, :], lambda b: x_sb[:, b, :], y0, "out_rows")

        @block.scalar
        def _(act):
            act.wait_ge(s["ones_ready"], 5)

            def exp_unit(c, j, u):
                act.wait_ge(s["least_ready"], 4 * c + j + 1)
                for r in range(QUADS):
                    ins = act.activation(p_sb[:, u, j, r, :], quad[2 + j % 2][:, r, :], ACT.Exp,
                                         bias=m_sb[:, u, j, r:r + 1], scale=-1.0)
                ins.then_inc(s["exped"], 1)

            def pT_copy(p, j, u):
                act.wait_ge(s["pT_done"], 4 * p + j + 1)
                if j == 0 and late(p, 2):
                    act.wait_ge(s["pv_done"], p - 1)
                act.copy(pT[:, u, j, :, :], quad[4 + j % 2]).then_inc(s["pT_copied"], 1)

            def v_copy(h):
                act.wait_ge(s["split_done"], 2 * h + 2)
                if late(h, 1):
                    act.wait_ge(s["v_placed"], h)
                act.copy(v_sb[:, :], bank[0][:, 2 * D:3 * D]).then_inc(s["v_copied"], 1)

            def step(t, u, layer, pair):
                h, c, p, o = t - 1, t - 2, t - 3, t - 4
                if late(o):
                    act.wait_ge(s["pv_done"], o + 1)
                    if late(o, 1):
                        act.wait_ge(s["o4_done"], o)
                    act.copy(oT[:, :, :], quad[6]).then_inc(s["oT_copied"], 1)
                if late(h):
                    act.wait_ge(s["xT_done"], h + 1)
                    if late(h, 1):
                        act.wait_ge(s["qkv_done"], h)
                    act.copy(xnT[:, :], bank[0][:, 384:512]).then_inc(s["xnT_copied"], 1)
                if late(c):
                    exp_unit(c, 0, u)
                if late(p):
                    pT_copy(p, 0, 1 - u)
                if late(o):
                    act.wait_ge(s["fT_done"], o + 1)
                    if late(o, 1):
                        act.wait_ge(s["proj_done"], o)
                    act.copy(ofT[:, :], bank[1][:, 0:128]).then_inc(s["fT_copied"], 1)
                if late(c):
                    exp_unit(c, 1, u)
                if late(p):
                    pT_copy(p, 1, 1 - u)
                if late(h):
                    act.wait_ge(s["q4T_done"], h + 1)
                    if late(h, 2):
                        act.wait_ge(s["s_done"], 4 * h - 4)
                    act.copy(q4[:, 1 - u, :, :], quad[1]).then_inc(s["q4_copied"], 1)
                if late(p):
                    pT_copy(p, 2, 1 - u)
                if late(h) and layer_of(h, layer) == 0:
                    v_copy(h)
                if late(c):
                    exp_unit(c, 2, u)
                if late(p):
                    pT_copy(p, 3, 1 - u)
                if late(c):
                    exp_unit(c, 3, u)
                if late(h):
                    act.wait_ge(s["kv_done"], h + 1)
                    act.copy(kv_sb[:, pair - 1 + u, 1 - u, :], bank[7][:, 0:D]).then_inc(s["kv_copied"], 1)

                if isinstance(t, int) and t > T:
                    y0T_copy(t - T - 1)
                if isinstance(t, int) and t == T + 3:
                    expert_copy(0)

            def y0T_copy(i):
                act.wait_ge(s["cm_ready"], B)
                act.wait_ge(s["f_xT_done"], i + 1)
                act.copy(y0T.rearrange("p b s -> p (b s)").rearrange("p (g b j) -> p b g j", b=B, j=NPOS)
                         [:, 4 * i:4 * i + 4],
                         bank[0].rearrange("p (b g j) -> p b g j", b=4, j=NPOS)).then_inc(s["f_xT_copied"], 1)

            def expert_copy(i):
                act.wait_ge(s["m_done"], i + 1)
                act.copy(mexp[:, 4 * i:4 * i + 4, :], quad[2 + i]).then_inc(s["m_copied"], 1)

            pipeline(act, step)
            expert_copy(1)
            y0T_copy(3)
            act.wait_ge(s["ffn_w_in"], 16 * nloads[0])
            act.wait_ge(s["w_ffq_ready"], 2)
            for i in range(4):
                act.wait_ge(s["qk_done"], 2 * i + 1)
                act.activation(qT[:, 4 * i:4 * i + 4, :], quad[2 * (i % 2)], ACT.Identity, bias=inb_col[:, 0:1])\
                   .then_inc(s["qT_ready"], 1)
                rows = slice(MHD * (MH - 1), MHD * MH)
                act.wait_ge(s["qk_done"], 2 * i + 2)
                if i % 2 == 0:
                    act.wait_ge(s["kblk_zeroed"], i // 2 + 1)
                act.activation(kblk(rows, 4 * i, 4)[:, :, MH - 1, :], quad[2 * (i % 2) + 1][rows], ACT.Identity,
                               bias=inb_col[rows, 1:2]).then_inc(s["k_last_ready"], 1)
                act.wait_ge(s["v_done"], i + 1)
                act.copy(vM[:, 4 * i:4 * i + 4, :], quad[4 + i]).then_inc(s["v_ready"], 1)

            for m in range(B + 4):
                if m < B:
                    act.wait_ge(s["f_least_ready"], m + 1)
                    for r in range(QUADS):
                        ins = act.activation(p_sb[:, (m // 4) % 2, m % 4, r, :], quad[m % 4][:, r, :], ACT.Exp,
                                             bias=m_sb[:, (m // 4) % 2, m % 4, r:r + 1], scale=-1.0)
                    ins.then_inc(s["f_exped"], 1)
                n = m - 3
                if 0 <= n < B:
                    act.wait_ge(s["f_pT_done"], n + 1)
                    if n >= 8:
                        act.wait_ge(s["f_pv_done"], n - 7)
                    act.copy(pT[:, (n // 4) % 2, n % 4, :, :], quad[4 + n % 2]).then_inc(s["f_pT_copied"], 1)
                if m == 3:
                    act.wait_ge(s["crep_done"], 1)
                    act.copy(crep[:, :], bank[7][:, 0:128]).then_inc(s["crep_copied"], 1)
                n = m - 4
                if n >= 0 and n % 4 == 3:
                    i = n // 4
                    act.wait_ge(s["f_pv_done"], n + 1)
                    act.activation(aT[:, :, 4 * NPOS * i:4 * NPOS * (i + 1)].rearrange("p b (r j) -> p r b j", r=QUADS),
                                   quad[6 + i % 2].rearrange("p r (b j) -> p r b j", j=NPOS), ACT.Identity,
                                   bias=inb_col[:, 2:3]).then_inc(s["aT_ready"], 1)
            for b in range(B):
                act.wait_ge(s["y1T_done"], b + 1)
                act.copy(y1T[:, b, :], bank[4 + b % 2][:, 0:128]).then_inc(s["y1T_copied"], 1)
            act.wait_ge(s["shifted"], 1)
            act.activation(lg[:, :, :], r_a[:, :, :], ACT.Exp).then_inc(s["gexp_ready"], 1)
            act.wait_ge(s["keptT_done"], 1)
            act.copy(keptT_bf[:, :], bank[4][:, 0:128]).then_inc(s["keptT_copied"], 1)
            act.copy(keptT[:, :], bank[4][:, 0:128]).then_inc(s["keptT_copied"], 1)

        @block.tensor
        def _(pe):
            pe.wait_ge(s["consts_in"], 48)
            pe.wait_ge(s["ones_ready"], 5)
            pe.wait_ge(s["attn_w_in"], 16)

            def s_unit(c, j, u, layer):
                if j == 0:
                    pe.wait_ge(s["q4_copied"], c + 1)
                    pe.wait_ge(s["k4_copied"], c + 1)
                    if isinstance(c, int) and c == B:
                        pe.wait_ge(s["mask_step"], 4)
                if late(c, 1) or j >= 2:
                    pe.wait_ge(s["exped"], 4 * c + j - 1)
                mask = xmask[:, batch(c, layer), :] if layer_of(c, layer) else causal[:, :]
                pe.matmul(quad[2 + j % 2], ident_bf[:, :], mask.unsqueeze(1).broadcast_to([128, QUADS, S]),
                          start=True, stop=False, skip_group_check=True)
                rows = slice(32 * j, 32 * j + 32)
                for r in range(QUADS):
                    mm = pe.matmul(quad[2 + j % 2][:, r, :], q4[rows, u, r, :], k4[rows, u, r, :],
                                   start=False, stop=True, skip_group_check=True)
                mm.then_inc(s["s_done"], 1)

            def pT_unit(p, j, u):
                pe.wait_ge(s["exped"], 4 * p + j + 1)
                if late(p, 1) or j >= 2:
                    pe.wait_ge(s["pT_copied"], 4 * p + j - 1)
                for r in range(QUADS):
                    mm = pe.transpose(bank[4 + j % 2][:, r * S:(r + 1) * S], p_sb[:, u, j, r, :], ident[:, :])
                mm.then_inc(s["pT_done"], 1)

            def project(h, u, layer):
                pe.wait_ge(s["xnT_copied"], h + 1)
                if isinstance(h, int) and h % B == 0:
                    pe.wait_ge(s["wq_ready"], h // B + 1)
                if layer_of(h, layer) == 0:
                    pe.matmul(bank[0][:, 0:3 * D], xnT[:, :], w_qkv_sb[:, :], start=True, stop=True)\
                      .then_inc(s["qkv_done"], 1)
                else:
                    pe.matmul(bank[0][:, 0:D], xnT[:, :], wq_sb[:, :], start=True, stop=True)\
                      .then_inc(s["qkv_done"], 1)

            def buckets_kv(h, u, pair, e0, e1):
                if e0 == 0:
                    if isinstance(h, int) and h == 0:
                        pe.wait_ge(s["xw_in"], 64)
                    pe.wait_ge(s["cm_ready"], pair + u)
                    if late(h, 3):
                        pe.wait_ge(s["o_ready"], h - 2)
                for e in range(e0, e1):
                    mm = pe.matmul(bank[7][:, 0:D], cm[:, e, :], wkv_sb[:, e, (1 - u) * D:(2 - u) * D],
                                   start=(e == 0), stop=(e == NBUCKET - 1))
                if e1 == NBUCKET:
                    mm.then_inc(s["kv_done"], 1)

            def step(t, u, layer, pair):
                h, c, p, o = t - 1, t - 2, t - 3, t - 4
                if late(h):
                    pe.wait_ge(s["xn_ready"], h + 1)
                    if late(h, 1):
                        pe.wait_ge(s["split_done"], 2 * h)
                        pe.wait_ge(s["v_copied"], min(h, B) if isinstance(h, int) else B if layer else h)
                    pe.transpose(bank[0][:, 384:512], xn[:, :], ident[:, :]).then_inc(s["xT_done"], 1)
                if late(c):
                    s_unit(c, 0, u, layer)
                if late(o):
                    pe.wait_ge(s["oT_copied"], o + 1)
                    if late(o, 1):
                        pe.wait_ge(s["kv_copied"], min(h, T) if isinstance(h, int) else h)
                    for r in range(QUADS):
                        mm = pe.transpose(quad[7][:, r, :], oT[:, r, :], ident[:, :])
                    mm.then_inc(s["o4_done"], 1)
                if late(p):
                    pT_unit(p, 0, 1 - u)
                if late(h):
                    project(h, 1 - u, layer)
                if late(c):
                    s_unit(c, 1, u, layer)
                if late(o):
                    pe.wait_ge(s["o_ready"], o + 1)
                    if late(h, 1):
                        pe.wait_ge(s["k4_copied"], h)
                    pe.transpose(bank[1][:, 0:128], o_sb[:, :], ident[:, :]).then_inc(s["fT_done"], 1)
                if late(p):
                    pT_unit(p, 1, 1 - u)
                if late(h):
                    buckets_kv(h, u, pair, 0, 4)
                if late(h):
                    pe.wait_ge(s["split_done"], 2 * h + 1)
                    if late(o):
                        pe.wait_ge(s["fT_copied"], o + 1)
                    if late(h, 1):
                        pe.wait_ge(s["k4_copied"], h)
                    for r in range(QUADS):
                        mm = pe.transpose(quad[1][:, r, :], qs[:, 4 * r:4 * r + 4, :, :, :]
                                          .rearrange("p j b a d -> p (j b a d)"), ident[:, :])
                    mm.then_inc(s["q4T_done"], 1)
                if late(c):
                    s_unit(c, 2, u, layer)
                if late(o):
                    pe.wait_ge(s["fT_copied"], o + 1)
                    lo = layer_of(o, layer)
                    mm = pe.matmul(bank[6][:, 0:D], ofT[:, :], w_out_sb[:, lo, :], start=True, stop=(lo == 0))
                    if lo:
                        mm = pe.matmul(bank[6][:, 0:D], ones_row[:, :], bo_row[:, :], start=False, stop=True)
                    mm.then_inc(s["proj_done"], 1)
                if late(p):
                    pT_unit(p, 2, 1 - u)
                if late(h):
                    pe.wait_ge(s["split_done"], 2 * h + 2)
                    pe.wait_ge(s["q4_copied"], h + 1)
                    for r in range(QUADS):
                        mm = pe.transpose(quad[1][:, r, :], ks[:, 4 * r:4 * r + 4, :, :, :]
                                          .rearrange("p j b a d -> p (j b a d)"), ident[:, :])
                    mm.then_inc(s["k4T_done"], 1)
                if late(p):
                    pT_unit(p, 3, 1 - u)
                if late(h):
                    buckets_kv(h, u, pair, 4, NBUCKET)
                if late(c):
                    s_unit(c, 3, u, layer)
                if late(p):
                    pe.wait_ge(s["pT_copied"], 4 * p + 4)
                    pe.wait_ge(s["v_placed"], p + 1)
                    if late(o):
                        pe.wait_ge(s["resid_done"], o + 1)
                    for r in range(QUADS):
                        for j in range(QUADS):
                            mm = pe.matmul(quad[6][32 * j:32 * j + 32, r, :], vaug[:, 1 - u, 4 * r + j, :],
                                           pT[:, 1 - u, j, r, :], start=True, stop=True, skip_group_check=True)
                    mm.then_inc(s["pv_done"], 1)

                if isinstance(t, int) and t > T:
                    y0T_quad(t - T - 1)
                if isinstance(t, int) and t == T + 2:
                    pe.wait_ge(s["exped"], 4 * T)
                    experts(0)

            def y0T_quad(i):
                if i == 0:
                    pe.wait_ge(s["split_done"], 2 * T)
                else:
                    pe.wait_ge(s["f_xT_copied"], i)
                for b in range(4 * i, 4 * i + 4):
                    pe.wait_ge(s["y0_ready"], b + 1)
                    mm = pe.transpose(quad[0][:, b % 4, :], y0[:, b, :], ident[:, :])
                mm.then_inc(s["f_xT_done"], 1)

            def experts(i):
                if i == 0:
                    pe.wait_ge(s["ffn_w_in"], 16 * nloads[0])
                for e in range(4 * i, 4 * i + 4):
                    for c in range(FC):
                        mm = pe.matmul(quad[2 + i][:, e % 4, :], w1t_sb[:, e, c, :], w2_sb[:, e, c, :],
                                       start=(c == 0), stop=(c == FC - 1))
                mm.then_inc(s["m_done"], 1)

            pipeline(pe, step)
            experts(1)
            pe.wait_ge(s["pT_copied"], 4 * T)
            for e in range(E):
                for c in range(FC):
                    mm = pe.matmul(bank[4][:, e:e + 1], w2_sb[:, e, c, :], b1t_sb[:, c, e:e + 1],
                                   start=(c == 0), stop=(c == FC - 1))
            mm.then_inc(s["cT_done"], 1)
            y0T_quad(3)
            pe.wait_ge(s["f_xT_copied"], 4)
            pe.wait_ge(s["m_copied"], 2)
            pe.wait_ge(s["w_ffq_ready"], 2)
            for i in range(4):
                if i >= 2:
                    pe.wait_ge(s["qT_ready"], i - 1)
                    pe.wait_ge(s["k_ready"], 3 * (i - 1))
                    pe.wait_ge(s["k_last_ready"], i - 1)
                for a in range(2):
                    pe.matmul(bank[2 * (i % 2) + a], inw_sb[:, a * D:(a + 1) * D], y0T[:, 4 * i:4 * i + 4, :],
                              start=True, stop=True).then_inc(s["qk_done"], 1)
                if i == 0:
                    pe.wait_ge(s["cT_ready"], 1)
                    pe.wait_ge(s["oT_copied"], T)
                    pe.wait_ge(s["resid_done"], T)
                for g in range(4 * i, 4 * i + 4):
                    mm = pe.matmul(quad[4 + i][:, g % 4, :], y0T[:, g, :], inw_sb[:, 2 * D:3 * D], start=True, stop=True)
                mm.then_inc(s["v_done"], 1)
            pe.wait_ge(s["qT_ready"], 4)
            pe.wait_ge(s["k_ready"], 12)
            pe.wait_ge(s["k_last_ready"], 4)
            pe.wait_ge(s["v_ready"], 4)
            for m in range(B + 4):
                if m < B:
                    if m >= 4:
                        pe.wait_ge(s["f_exped"], m - 3)
                    pe.matmul(quad[m % 4], ident_bf[:, :], samepos[:, :].unsqueeze(1).broadcast_to([128, QUADS, 128]),
                              start=True, stop=False, skip_group_check=True)
                    pe.matmul(quad[m % 4], qT[:, m, :], kblk(slice(0, 128), m, 1)[:, 0], start=False, stop=True,
                              skip_group_check=True).then_inc(s["f_s_done"], 1)
                if m == 2:
                    pe.wait_ge(s["crepT_ready"], 1)
                    pe.transpose(bank[7][:, 0:128], crepT[:, :, :].rearrange("p b e -> p (b e)"), ident[:, :])\
                      .then_inc(s["crep_done"], 1)
                n = m - 3
                if 0 <= n < B:
                    pe.wait_ge(s["f_divided"], n + 1)
                    if n >= 2:
                        pe.wait_ge(s["f_pT_copied"], n - 1)
                    for r in range(QUADS):
                        mm = pe.transpose(quad[4 + n % 2][:, r, :], p_sb[:, (n // 4) % 2, n % 4, r, :], ident[:, :])
                    mm.then_inc(s["f_pT_done"], 1)
                n = m - 4
                if n >= 0:
                    i = n // 4
                    pe.wait_ge(s["f_pT_copied"], n + 1)
                    if i == 1:
                        pe.wait_ge(s["crep_copied"], 1)
                    if i >= 2:
                        pe.wait_ge(s["aT_ready"], i - 1)
                    for j in range(MH):
                        mm = pe.matmul(quad[6 + i % 2][MHD * j:MHD * (j + 1), n % 4, :], vM[:, n, MHD * j:MHD * (j + 1)],
                                       pT[:, i % 2, n % 4, j, :], start=True, stop=True, skip_group_check=True)
                    mm.then_inc(s["f_pv_done"], 1)
            pe.wait_ge(s["aT_ready"], 4)
            for m in range(B + 7):
                if m < B:
                    if m >= 4:
                        pe.wait_ge(s["z_ready"], m - 3)
                    pe.matmul(bank[m % 4][:, 0:D], aT[:, m, :], ow_sb[:, :], start=True, stop=False)
                    pe.matmul(bank[m % 4][:, 0:D], ones_row[:, :], ob_row[:, :], start=False, stop=True)\
                      .then_inc(s["f_proj_done"], 1)
                b = m - 6
                if 0 <= b < B:
                    if b >= 2:
                        pe.wait_ge(s["y1T_copied"], b - 1)
                    pe.wait_ge(s["y1_ready"], b + 1)
                    pe.transpose(bank[4 + b % 2][:, 0:128], y1[:, b, :], ident[:, :]).then_inc(s["y1T_done"], 1)
                b = m - 7
                if b >= 0:
                    pe.wait_ge(s["y1T_copied"], b + 1)
                    pe.matmul(bank[6][:, b * E:(b + 1) * E], y1T[:, b, :], wg_sb[:, :], start=True, stop=True)\
                      .then_inc(s["logits_done"], 1)
            pe.wait_ge(s["pick_ready"], 1)
            picks = pick_bf[:, :, :].rearrange("p b e -> p (b e)")
            pe.matmul(bank[7][:, 0:B * E], before[:, :], picks, start=True, stop=False, skip_group_check=True)
            for k in range(1, B):
                mm = pe.matmul(bank[7][:, k * E:B * E], ones_bf[:, :], picks[:, 0:(B - k) * E], start=False, stop=(k == B - 1),
                               skip_group_check=True)
            mm.then_inc(s["place_done"], 1)
            pe.wait_ge(s["kept_ready"], 1)
            pe.transpose(bank[4][:, 0:128], kept[:, :, :].rearrange("p b e -> p (b e)"), ident[:, :]).then_inc(s["keptT_done"], 1)
            pe.wait_ge(s["keptT_copied"], 2)
            pe.wait_ge(s["cblk_ready"], 1)
            for m in range(B + 1):
                if m < B:
                    if m >= 2:
                        pe.wait_ge(s["gated"], m - 1)
                    for e in range(E):
                        row = m * E + e
                        mm = pe.matmul(quad[2 * (m % 2) + e // 4][:, e % 4, :], ident_bf[:, row:row + 1].broadcast_to([128, 128]),
                                       keptT_bf[:, :], start=True, stop=True)
                    mm.then_inc(s["hot_done"], 1)
                b = m - 1
                if b >= 0:
                    pe.wait_ge(s["gated"], b + 1)
                    if b >= 4:
                        pe.wait_ge(s["z_ready"], B + b - 3)
                    for e in range(E):
                        pe.matmul(bank[4 + b % 4][:, 0:D], prod[:, b % 2, e, :], mexp[:, e, :], start=(e == 0), stop=False)
                    pe.matmul(bank[4 + b % 4][:, 0:D], keptT[:, :], cblk[:, b, :], start=False, stop=True)\
                      .then_inc(s["ffn_done"], 1)




def kernel(**inputs):
    import numpy as _np
    import concourse.bacc as _bacc
    from concourse import mybir as _mybir
    from concourse.bass_utils import run_bass_kernel_spmd as _run

    a = {k: _np.asarray(v) for k, v in inputs.items()}
    import ml_dtypes
    bf = ml_dtypes.bfloat16
    p = _np.arange(128)
    arrays = {
        "x": a["x"],
        "ctxT": a["ctx_1024"].transpose(0, 2, 1),
        "fside": a["fside_BxS2_0"],
        "fsideT": a["fside_BxS2_0"].T,
        "itok": a["itok_BxS2_0_7"],
        "pad": a["mask_BxS2_bf0"].view(_np.int32),
        "w_qkv": a["L0_attn_w_qkv"],
        "w_out": a["L0_attn_w_out"],
        "wq": a["L0_xattn_Wq"],
        "wkv": _np.concatenate([a["L0_xattn_Wk_b"], a["L0_xattn_Wv_b"]], axis=2),
        "wo": a["L0_xattn_Wo"],
        "bo": a["L0_xattn_bo"][None],
        "inw": a["L0_ffn_in_proj_w"].T,
        "inb": a["L0_ffn_in_proj_b"].reshape(3, D).T,
        "ow": a["L0_ffn_out_proj_w"].T,
        "ob": a["L0_ffn_out_proj_b"][None],
        "g1": a["L0_ffn_ln1_g"],
        "be1": a["L0_ffn_ln1_b"],
        "g2": a["L0_ffn_ln2_g"],
        "be2": a["L0_ffn_ln2_b"],
        "wg": a["L0_ffn_wg"],
        "w1t": a["L0_ffn_w1"].transpose(0, 2, 1),
        "b1t": a["L0_ffn_b1"].T,
        "w2": a["L0_ffn_w2"],
        "b2t": a["L0_ffn_b2"].T,
        "c_ident": _np.eye(128, dtype=_np.float32),
        "c_ident_bf": _np.eye(128, dtype=bf),
        "c_causal": _np.where(p[:, None] >= p[None, :], 0.0, MASKED).astype(bf),
        "c_samepos": _np.where(p[:, None] % 8 == p[None, :] % 8, 0.0, MASKED).astype(bf),
        "c_before": (p[:, None] < p[None, :]).astype(bf),
        "c_rank": _np.broadcast_to(_np.arange(E, 0, -1, dtype=_np.float32), (128, B, E)),
        "c_batchof": (p[:, None] // E == _np.arange(B)[None, :]).astype(_np.float32),
    }
    arrays = {k: _np.ascontiguousarray(v) for k, v in arrays.items()}
    nc = _bacc.Bacc("TRN2", target_bir_lowering=False, num_devices=1)
    args = {k: nc.dram_tensor(k, v.shape, _mybir.dt.from_np(v.dtype), kind="ExternalInput").ap()
            for k, v in arrays.items()}
    out = nc.dram_tensor("out", (B, S, D), _mybir.dt.float32, kind="ExternalOutput").ap()
    decoder_kernel(nc, **args, out=out)
    r = _run(nc, [arrays], core_ids=[0])
    return r.results[0]["out"]
```

```python
import numpy as np
import concourse.bass as bass
from concourse import mybir
from contextlib import ExitStack

B, S, D = 16, 128, 128
H, HD = 16, 8
NBUCKET = 8
MH, MHD = 4, 32
E, FF = 8, 512
CAP = B * S // E
EPS = 1e-5
MASKED = float(2 ** 100)
FAR = 3e38
QUADS = 4
LAGS = 4
PEEL = 6


def decoder_kernel(nc, x, ctxT, fside, fsideT, itok, pad, w_qkv, w_out, wq, wkv, wo, bo,
                   inw, inb, ow, ob, g1, be1, g2, be2, wg, w1t, b1t, w2, b2,
                   c_ident, c_ident_bf, c_odd_even, c_causal, c_samepos, c_before, c_rank,
                   c_batchof, c_pick_expert, out):
    f32, f32r, bf16 = mybir.dt.float32, mybir.dt.float32r, mybir.dt.bfloat16
    ALU, ACT, AX = mybir.AluOpType, mybir.ActivationFunctionType, mybir.AxisListType
    FC = FF // 128
    T = 2 * B
    nloads = [0]
    NPOS = S // B

    st = ExitStack()
    with st:
        def sb(name, shape, dt=f32):
            return st.enter_context(nc.sbuf_tensor(name, shape, dt))

        def sem(name):
            return st.enter_context(nc.semaphore(name))

        w_qkv_sb = sb("w_qkv_sb", [128, 3 * D])
        w_out_sb = sb("w_out_sb", [128, 2, D])
        wq_sb = sb("wq_sb", [128, D])
        wkv_sb = sb("wkv_sb", [128, NBUCKET, 2 * D])
        bo_rows = sb("bo_rows", [128, D])
        inw_sb = sb("inw_sb", [128, 3 * D])
        inb_col = sb("inb_col", [128, 3])
        ow_sb = sb("ow_sb", [128, D])
        ob_rows = sb("ob_rows", [128, D])
        ln_rows = sb("ln_rows", [128, 4, D])
        wg_sb = sb("wg_sb", [128, E])
        w1t_sb = sb("w1t_sb", [128, E, FC, D])
        w2_sb = sb("w2_sb", [128, E, FC, D])
        b1t_sb = sb("b1t_sb", [128, FC, E])
        b2_sb = sb("b2_sb", [E, D])
        ident = sb("ident", [128, 128])
        causal = sb("causal", [128, 128], bf16)
        ident_bf = sb("ident_bf", [128, 128], bf16)
        samepos = sb("samepos", [128, 128], bf16)
        before = sb("before", [128, 128], bf16)
        ones_bf = sb("ones_bf", [128, 128], bf16)
        rank = sb("rank", [128, B, E])
        batchof = sb("batchof", [128, B])
        x_sb = sb("x_sb", [128, B, D])
        ctx_sb = sb("ctx_sb", [128, B, S])
        itok_i = sb("itok_i", [128, B, S], mybir.dt.int32)
        itok_bf = sb("itok_bf", [128, B, S], bf16)
        onehot = sb("onehot", [128, NBUCKET, B, S], bf16)
        tk = sb("tk", [128, B, S])
        tq = sb("tq", [128, B])
        pad_words = sb("pad_words", [128, B, S // 4], mybir.dt.int32)
        y1T = sb("y1T", [128, B, S])
        xmask = y1T[:, :, :].rearrange("p b s -> p (b s)").bitcast(bf16)[:, 0:B * S]\
            .rearrange("p (b s) -> p b s", b=B)

        stats = sb("stats", [128, 6])
        mv = sb("mv", [128, 2])
        veps = sb("veps", [128, 1])
        minus_half = sb("minus_half", [128, 1])
        rstd = sb("rstd", [128, 1])
        xn = sb("xn", [128, D])
        xnT = sb("xnT", [128, S])
        cm = sb("cm", [128, NBUCKET, S])
        kv_sb = sb("kv_sb", [128, B, 2, D])
        qs, ks = (w2_sb[:, e, :, :].rearrange("p c d -> p (c d)") for e in (E - 2, E - 1))
        qs = qs.rearrange("p (h b a d) -> p h b a d", h=H, b=2, a=2)
        ks = ks.rearrange("p (h a b d) -> p h a b d", h=H, b=2, a=2)
        q4 = sb("q4", [128, 2, QUADS, S], f32r)
        k4 = sb("k4", [128, 2, QUADS, 2, S], f32r)
        odd_even = sb("odd_even", [128, 2])
        mask_now = sb("mask_now", [128, 2, S], bf16)
        v_sb = sb("v_sb", [128, D])
        vaug = sb("vaug", [128, 2, H, 32])
        p_sb = sb("p_sb", [128, 2, QUADS, QUADS, S])
        m_sb = sb("m_sb", [128, 2, QUADS, QUADS])
        pT = sb("pT", [128, 2, QUADS, QUADS, S])
        oT = sb("oT", [128, QUADS, S])
        rden = sb("rden", [128, QUADS, QUADS])
        o_sb = sb("o_sb", [128, D])
        ofT = sb("ofT", [128, S])

        free = onehot[:, :, :, :].rearrange("p e b s -> p (e b s)").bitcast(f32)
        spans = [free[:, i * B * S:(i + 1) * B * S].rearrange("p (b s) -> p b s", b=B) for i in range(4)]
        y0T, qT, z16, aT = spans
        y0 = itok_i[:, :, :].bitcast(f32)
        y1 = tk[:, :, :]
        vM = ctx_sb[:, :, :]
        prod = pT[:, :, :, :, :].rearrange("p u j r q -> p u (j r q)")[:, :, 0:E * D]\
            .rearrange("p u (e d) -> p u e d", e=E)
        mexp = cm[:, :, :]
        cblk = p_sb[:, 0, :, :, :].rearrange("p j r k -> p (j r) k")
        pick_expert = itok_bf[0:E, :, :].rearrange("p b s -> p (b s)").bitcast(f32)\
            .rearrange("p (e r) -> p e r", e=E)
        pick_all = sb("pick_all", [E, 128])
        st16 = sb("st16", [128, B, 6])
        mv16 = sb("mv16", [128, B, 2])
        ve16 = sb("ve16", [128, B])
        half16 = sb("half16", [128, B])
        rs16 = sb("rs16", [128, B])
        spare = wkv_sb[:, :, :].rearrange("p e n -> p (e n)")
        used = [0]

        def over_wkv(n, *dims):
            used[0] += n
            part = spare[:, used[0] - n:used[0]]
            return part.rearrange("p (a b) -> p a b", b=dims[0]) if dims else part

        dsum = over_wkv(4 * MH * QUADS, QUADS)
        drec = over_wkv(4 * MH * QUADS, QUADS)
        lg, r_a, r_b = (over_wkv(B * E, E) for _ in range(3))
        r_m, r_s = over_wkv(B), over_wkv(B)
        gate = over_wkv(B)
        kept = over_wkv(B * E, E)
        keptT = over_wkv(128)
        crep = over_wkv(D)
        b1w2 = over_wkv(E * D, D)
        keptT_bf = sb("keptT_bf", [128, 128], bf16)
        pick_bf = sb("pick_bf", [128, B, E], bf16)

        def kblk(rows, g, n):
            half = (kv_sb, w1t_sb)[g // 8][rows, :, :, :].rearrange("p a b c -> p (a b c)")\
                .rearrange("p (g j s) -> p g j s", g=B // 2, j=MH)
            return half[:, g % 8:g % 8 + n]

        ps = st.enter_context(nc.psum_tensor("ps", [128, 8, 512], f32))
        bank = [ps[:, i, :] for i in range(8)]
        quad = [b.rearrange("p (r k) -> p r k", r=QUADS) for b in bank]

        names = """last_w2_in ident_in consts_in itok_in wkv_in times_in x_in x_rest_in wqkv_in attn_w_in ctx_in xw_in
            ffn_w_in ones_ready bn_step veps_ready pow_done xn_ready xT_done xnT_copied qkv_done hi_done
            split_done v_copied v_placed q4T_done q4_copied k4T_done k4_copied s_done least_ready subbed
            even_exped odd_exped wq_ready w_ffq_ready pT_done pT_copied pv_done oT_copied o4_done den_done
            o_ready fT_done fT_copied proj_done resid_done itok_ready onehot_step mask_step mask_now_ready
            scores_seen cm_ready kv_done kv_copied stored m_done m_copied cb_done b1w2_ready crep_done
            crep_copied st_step mv_step ve_ready rs_ready y0_ready y0_biased bo_added f_xT_done f_xT_copied
            qk_done qT_ready kblk_zeroed k_ready k_last_ready v_done v_ready f_s_done f_least_ready f_exped
            f_sum f_drec f_divided f_pT_done f_pT_copied f_pv_done aT_ready f_proj_done z_ready w_ready y1_ready
            y1T_done y1T_copied logits_done route_step shifted gexp_ready pick_ready gate_ready place_done
            kept_ready keptT_done keptT_copied cblk_ready xb_ready hot_done gated ffn_done out_rows""".split()
        assert len(names) == len(set(names))
        s = {n: sem(n) for n in names}
        block = st.enter_context(nc.Block())

        def late(k, n=0):
            return not isinstance(k, int) or n <= k < T

        def kv_halves(t):
            if isinstance(t, int) and t < PEEL:
                return {3: [0, 1], 4: [2, 3], 5: [4]}.get(t, [])
            return [t - 1] if late(t - 1) else []

        def layer_of(k, layer):
            return layer if not isinstance(k, int) else int(k >= B)

        def batch(k, layer):
            return k - B if layer_of(k, layer) else k

        def pipeline(e, step):
            for layer in range(2):
                for t in range(layer * B, layer * B + PEEL):
                    step(t, t % 2, layer, t // 2)
                with e.Fori((layer * B + PEEL) // 2, (layer + 1) * B // 2) as i:
                    step(2 * i, 0, layer, i)
                    step(2 * i + 1, 1, layer, i)
            for t in range(T, T + LAGS):
                step(t, t % 2, 1, t // 2)

        def bcast(v):
            return v.unsqueeze(2).broadcast_to([128, B, E])


        @block.sync
        def _(sp):
            sp.dma_start(x_sb[:, 0:4, :], x[0:4].rearrange("b s d -> s b d")).then_inc(s["x_in"], 16)
            sp.dma_start(w_qkv_sb[:, :], w_qkv).then_inc(s["wqkv_in"], 16)
            sp.dma_start(ident[:, :], c_ident).then_inc(s["ident_in"], 16)
            sp.dma_start(causal[:, :], c_causal).then_inc(s["consts_in"], 16)
            sp.dma_start(ident_bf[:, :], c_ident_bf).then_inc(s["consts_in"], 16)
            sp.dma_start(odd_even[:, :], c_odd_even).then_inc(s["consts_in"], 16)
            sp.dma_start(x_sb[:, 4:B, :], x[4:B].rearrange("b s d -> s b d")).then_inc(s["x_rest_in"], 16)
            sp.dma_start(itok_i[:, :, :], itok.partition_broadcast(128)).then_inc(s["itok_in"], 16)
            sp.dma_start(ctx_sb[:, :, :], ctxT.rearrange("b d s -> d b s")).then_inc(s["ctx_in"], 16)
            sp.dma_start(wkv_sb[:, :, :], wkv.rearrange("e d n -> d e n")).then_inc(s["wkv_in"], 16)
            sp.dma_start(w_out_sb[:, 0, :], w_out).then_inc(s["attn_w_in"], 16)
            sp.dma_start(tk[:, :, :], fside.partition_broadcast(128)).then_inc(s["times_in"], 16)
            sp.dma_start(tq[:, :], fsideT).then_inc(s["times_in"], 16)
            sp.dma_start(pad_words[:, :, :], pad.partition_broadcast(128)).then_inc(s["times_in"], 16)
            sp.dma_start(wq_sb[:, :], wq).then_inc(s["xw_in"], 16)
            sp.dma_start(w_out_sb[:, 1, :], wo).then_inc(s["xw_in"], 16)
            sp.dma_start(bo_rows[:, :], bo.partition_broadcast(128)).then_inc(s["xw_in"], 16)
            loads = [(w1t_sb[:, :, :, :], w1t.rearrange("e (c p) d -> p e c d", p=128)),
                     (w2_sb[:, 0:E - 2, :, :], w2[0:E - 2].rearrange("e (c p) d -> p e c d", p=128)),
                     (b1t_sb[:, :, :], b1t.rearrange("(c p) e -> p c e", p=128)), (b2_sb[:, :], b2),
                     (inw_sb[:, :], inw), (inb_col[:, :], inb), (ow_sb[:, :], ow),
                     (ob_rows[:, :], ob.partition_broadcast(128)),
                     (wg_sb[:, :], wg), (samepos[:, :], c_samepos), (before[:, :], c_before),
                     (rank[:, :, :], c_rank), (batchof[:, :], c_batchof),
                     (pick_all[:, :], c_pick_expert[:, E, :])]
            loads += [(ln_rows[:, i, :], v.partition_broadcast(128)) for i, v in enumerate((g1, be1, g2, be2))]
            for dst, src in loads:
                sp.dma_start(dst, src).then_inc(s["ffn_w_in"], 16)
            sp.wait_ge(s["onehot_step"], 4 * NBUCKET)
            sp.dma_start(pick_expert, c_pick_expert[:, 0:E, :]).then_inc(s["ffn_w_in"], 16)
            nloads[0] = len(loads) + 1
            sp.wait_ge(s["k4T_done"], T)
            sp.dma_start(w2_sb[:, E - 2:E, :, :], w2[E - 2:E].rearrange("e (c p) d -> p e c d", p=128))\
              .then_inc(s["last_w2_in"], 16)
            for i in range(B // 2):
                sp.wait_ge(s["out_rows"], 2 * i + 2)
                sp.dma_start(out[2 * i:2 * i + 2].rearrange("b s d -> s b d"), y0[:, 2 * i:2 * i + 2, :])\
                  .then_inc(s["stored"], 16)
            sp.wait_ge(s["stored"], 16 * (B // 2))

        @block.vector
        def _(dve):
            dve.memset(vaug[:, :, :, :], 1.0).then_inc(s["ones_ready"], 1)
            dve.memset(minus_half[:, :], -0.5).then_inc(s["ones_ready"], 1)
            dve.memset(half16[:, :], -0.5).then_inc(s["ones_ready"], 1)
            dve.memset(ones_bf[:, :], 1.0).then_inc(s["ones_ready"], 1)
            dve.wait_ge(s["wqkv_in"], 16)
            dve.tensor_scalar(w_qkv_sb[:, 0:D], w_qkv_sb[:, 0:D], -HD ** -0.5, None, ALU.mult)\
               .then_inc(s["wq_ready"], 1)
            dve.wait_ge(s["x_in"], 16)

            def norm_stats(t, layer):
                dve.bn_stats(stats[:, :], x_sb[:, batch(t, layer), :]).then_inc(s["bn_step"], 1)

            def norm_variance(t):
                if isinstance(t, int):
                    dve.wait_ge(s["bn_step"], 2 * t + 1)
                    if t >= 1:
                        dve.wait_ge(s["xn_ready"], t)
                dve.bn_aggr(mv[:, :], stats[:, :]).then_inc(s["bn_step"], 1)
                dve.wait_ge(s["bn_step"], 2 * t + 2)
                if late(t, 1):
                    dve.wait_ge(s["pow_done"], t)
                dve.tensor_scalar(veps[:, :], mv[:, 1:2], EPS, None, ALU.add).then_inc(s["veps_ready"], 1)

            def norm_rows(t, layer):
                dve.wait_ge(s["pow_done"], t + 1)
                if late(t, 1):
                    dve.wait_ge(s["xT_done"], t)
                dve.tensor_scalar(xn[:, :], x_sb[:, batch(t, layer), :], mv[:, 0:1], rstd[:, :],
                                  ALU.subtract, ALU.mult).then_inc(s["xn_ready"], 1)

            def split(h, layer):
                dve.wait_ge(s["qkv_done"], h + 1)
                q, k = bank[0][:, 0:D], bank[0][:, D:2 * D]
                if layer_of(h, layer):
                    dve.wait_ge(s["kv_copied"], 2 * (h - B) + 1)
                    k = kv_sb[:, h - B, 0, :]
                q, k = (a.rearrange("p (h d) -> p h d", d=HD).unsqueeze(2).broadcast_to([128, H, 2, HD])
                        for a in (q, k))
                if late(h, 1):
                    dve.wait_ge(s["k4T_done"], h)
                dve.tensor_copy(qs[:, :, :, 0, :].bitcast(f32r), q).then_inc(s["hi_done"], 1)
                dve.tensor_copy(ks[:, :, 0, :, :].bitcast(f32r), k).then_inc(s["hi_done"], 1)
                dve.wait_ge(s["hi_done"], 2 * h + 1)
                dve.tensor_tensor(qs[:, :, :, 1, :], q, qs[:, :, :, 0, :], ALU.subtract).then_inc(s["split_done"], 1)
                dve.wait_ge(s["hi_done"], 2 * h + 2)
                dve.tensor_tensor(ks[:, :, 1, :, :], k, ks[:, :, 0, :, :], ALU.subtract).then_inc(s["split_done"], 1)

            def step_mask(c, u, layer):
                if isinstance(c, int) and c == B:
                    dve.wait_ge(s["mask_step"], 3)
                dve.tensor_copy(mask_now[:, u, :], xmask[:, batch(c, layer), :]).then_inc(s["mask_now_ready"], 1)
                dve.wait_ge(s["mask_now_ready"], c - B + 1)

            def unit(c, j, u, layer):
                if j == 0 and layer_of(c, layer):
                    step_mask(c, u, layer)
                mask = mask_now[:, u, :] if layer_of(c, layer) else causal[:, :]
                dve.wait_ge(s["s_done"], 4 * c + j + 1)
                if j == 0 and late(c, 2):
                    dve.wait_ge(s["even_exped"], 2 * c - 2)
                    dve.wait_ge(s["subbed"], 2 * c - 2)
                if isinstance(c, int) and c == 0:
                    dve.wait_ge(s["consts_in"], 48)
                if j % 2 and late(c, 2):
                    dve.wait_ge(s["pT_done"], 4 * c + j - 7)
                dve.sem_inc(s["scores_seen"], 1)
                for r in range(QUADS):
                    scores = quad[2 + j % 2][:, r, :]
                    ins = dve.tensor_tensor_reduce(p_sb[:, u, j, r, :] if j % 2 else scores, scores, mask, 1.0, FAR,
                                                   ALU.add, ALU.min, accum_out=m_sb[:, u, j, r:r + 1])
                ins.then_inc(s["least_ready"], 1)

            def k4_copy(h, u):
                if isinstance(h, int) and h == 0:
                    dve.wait_ge(s["consts_in"], 48)
                dve.wait_ge(s["k4T_done"], h + 1)
                if late(h, 2):
                    dve.wait_ge(s["s_done"], 4 * h - 4)
                dve.tensor_tensor(k4[:, u, :, :, :], quad[1].unsqueeze(2).broadcast_to([128, QUADS, 2, S]),
                                  odd_even[:, :].unsqueeze(1).unsqueeze(3).broadcast_to([128, QUADS, 2, S]),
                                  ALU.mult).then_inc(s["k4_copied"], 1)

            def divide(o):
                dve.wait_ge(s["o4_done"], o + 1)
                o4 = bank[7].rearrange("p (r j c) -> p r j c", r=QUADS, j=QUADS)
                dve.reciprocal(rden[:, :, :], o4[:, :, :, HD]).then_inc(s["den_done"], 1)
                dve.wait_ge(s["den_done"], o + 1)
                if late(o, 1):
                    dve.wait_ge(s["fT_done"], o)
                dve.tensor_tensor(o_sb[:, :].rearrange("p (r j c) -> p r j c", r=QUADS, j=QUADS),
                                  o4[:, :, :, 0:HD],
                                  rden[:, :, :].unsqueeze(3).broadcast_to([128, QUADS, QUADS, HD]),
                                  ALU.mult).then_inc(s["o_ready"], 1)

            def residual(f, layer):
                if layer_of(f, layer):
                    dve.wait_ge(s["bo_added"], f - B + 1)
                dve.wait_ge(s["proj_done"], f + 1)
                rows = x_sb[:, batch(f, layer), :]
                dve.tensor_tensor(rows, rows, bank[6][:, 0:D], ALU.add).then_inc(s["resid_done"], 1)

            def step(t, u, layer, pair):
                h, c, o = t - 1, t - 2, t - 4
                if isinstance(t, int) and t == 4:
                    dve.wait_ge(s["x_rest_in"], 16)
                if late(t):
                    norm_stats(t, layer)
                if isinstance(t, int) and t == B:
                    dve.wait_ge(s["xw_in"], 48)
                    dve.tensor_scalar(wq_sb[:, :], wq_sb[:, :], -HD ** -0.5, None, ALU.mult)\
                       .then_inc(s["wq_ready"], 1)
                if late(c):
                    unit(c, 0, u, layer)
                if late(o):
                    divide(o)
                if late(h):
                    split(h, layer)
                if late(c):
                    unit(c, 1, u, layer)
                if late(t):
                    norm_variance(t)
                if late(c):
                    unit(c, 2, u, layer)
                if late(t):
                    norm_rows(t, layer)
                if isinstance(t, int) and t > T:
                    y0_rows(t - T - 1)
                if isinstance(t, int) and 2 <= t < 6:
                    one_hots(t - 2)
                if isinstance(t, int) and t == T:
                    y0_variance(0, B - 4)
                if late(o):
                    residual(o, layer)
                if late(h):
                    k4_copy(h, 1 - u)
                if late(c):
                    unit(c, 3, u, layer)
                if isinstance(t, int) and 3 <= t < 6:
                    mask_part(t - 3)

            def one_hots(i):
                if i == 0:
                    dve.wait_ge(s["itok_in"], 16)
                    dve.tensor_copy(itok_bf[:, :, :], itok_i[:, :, :]).then_inc(s["itok_ready"], 1)
                    dve.wait_ge(s["itok_ready"], 1)
                for e in range(NBUCKET):
                    dve.tensor_scalar(onehot[:, e, 4 * i:4 * i + 4, :], itok_bf[:, 4 * i:4 * i + 4, :],
                                      float(e), None, ALU.is_equal).then_inc(s["onehot_step"], 1)

            def mask_part(part):
                if part == 0:
                    dve.wait_ge(s["times_in"], 16 * 3)
                    ins = dve.tensor_tensor(tk[:, :, :], tk[:, :, :],
                                            tq[:, :].unsqueeze(2).broadcast_to([128, B, S]), ALU.is_gt)
                else:
                    dve.wait_ge(s["mask_step"], part)
                if part == 1:
                    ins = dve.tensor_tensor(tk[:, :, :], tk[:, :, :], pad_words[:, :, :].bitcast(mybir.dt.uint8),
                                            ALU.max)
                if part == 2:
                    ins = dve.tensor_scalar(xmask, tk[:, :, :], -MASKED, MASKED, ALU.mult, ALU.add)
                ins.then_inc(s["mask_step"], 1)

            def y0_variance(b0, b1):
                dve.wait_ge(s["resid_done"], B + b1)
                for b in range(b0, b1):
                    dve.bn_stats(st16[:, b, :], x_sb[:, b, :]).then_inc(s["st_step"], 1)
                dve.wait_ge(s["st_step"], b1)
                for b in range(b0, b1):
                    dve.bn_aggr(mv16[:, b, :], st16[:, b, :]).then_inc(s["mv_step"], 1)
                dve.wait_ge(s["mv_step"], b1)
                dve.tensor_scalar(ve16[:, b0:b1], mv16[:, b0:b1, 1], EPS, None, ALU.add).then_inc(s["ve_ready"], 1)

            def y0_rows(i):
                dve.wait_ge(s["rs_ready"], 2 if i == 3 else 1)
                for b in range(4 * i, 4 * i + 4):
                    dve.tensor_scalar(y0[:, b, :], x_sb[:, b, :], mv16[:, b, 0:1], rs16[:, b:b + 1],
                                      ALU.subtract, ALU.mult).then_inc(s["y0_ready"], 1)

            pipeline(dve, step)
            y0_variance(B - 4, B)
            y0_rows(3)
            dve.wait_ge(s["ffn_w_in"], 16 * nloads[0])
            dve.tensor_scalar(inw_sb[:, 0:D], inw_sb[:, 0:D], -MHD ** -0.5, None, ALU.mult)\
                .then_inc(s["w_ffq_ready"], 1)
            dve.tensor_scalar(inb_col[:, 0:1], inb_col[:, 0:1], -MHD ** -0.5, None, ALU.mult)\
                .then_inc(s["w_ffq_ready"], 1)
            for i in range(4):
                dve.wait_ge(s["qk_done"], 2 * i + 2)
                if i % 2 == 0:
                    dve.wait_ge(s["kblk_zeroed"], i // 2 + 1)
                for j in range(MH - 1):
                    rows = slice(MHD * j, MHD * (j + 1))
                    dve.tensor_scalar(kblk(rows, 4 * i, 4)[:, :, j, :], quad[2 * (i % 2) + 1][rows],
                                      inb_col[rows, 1:2], None, ALU.add).then_inc(s["k_ready"], 1)

            def mha_sum(n):
                dve.wait_ge(s["f_exped"], n + 1)
                dve.tensor_reduce(dsum[:, n, :], p_sb[:, (n // 4) % 2, n % 4, :, :], AX.X, ALU.add)\
                    .then_inc(s["f_sum"], 1)
                dve.wait_ge(s["f_sum"], n + 1)
                dve.reciprocal(drec[:, n, :], dsum[:, n, :]).then_inc(s["f_drec"], 1)

            for n in range(B):
                dve.wait_ge(s["f_s_done"], n + 1)
                dve.tensor_reduce(m_sb[:, (n // 4) % 2, n % 4, :], quad[n % 4], AX.X, ALU.min)\
                    .then_inc(s["f_least_ready"], 1)
                if n >= 1:
                    mha_sum(n - 1)
            mha_sum(B - 1)

            def z_stats(b, k):
                dve.wait_ge(s["z_ready"], B * k + b + 1)
                dve.bn_stats(st16[:, b, :], z16[:, b, :]).then_inc(s["st_step"], 1)

            def pair_variance(b, k):
                dve.wait_ge(s["st_step"], B * (k + 1) + b + 1)
                for a in (b - 1, b):
                    dve.bn_aggr(mv16[:, a, :], st16[:, a, :]).then_inc(s["mv_step"], 1)
                dve.wait_ge(s["mv_step"], B * (k + 1) + b + 1)
                dve.tensor_scalar(ve16[:, b - 1:b + 1], mv16[:, b - 1:b + 1, 1], EPS, None, ALU.add)\
                    .then_inc(s["ve_ready"], 1)

            def z_scaled(b, k, scale):
                dve.wait_ge(s["mv_step"], B * (k + 1) + b + 1)
                dve.scalar_tensor_tensor(z16[:, b, :], z16[:, b, :], mv16[:, b, 0:1], scale, ALU.subtract, ALU.mult)\
                   .then_inc(s["w_ready"], 1)

            def z_rows(b, k, bias, dst, done):
                dve.wait_ge(s["rs_ready"], 2 + k * (B // 2) + b // 2 + 1)
                dve.wait_ge(s["w_ready"], B * k + b + 1)
                dve.scalar_tensor_tensor(dst[:, b, :], z16[:, b, :], rs16[:, b:b + 1], bias, ALU.mult, ALU.add)\
                   .then_inc(s[done], 1)

            for b in range(B + 3):
                if b < B:
                    if b == 0:
                        dve.wait_ge(s["y0_biased"], 1)
                    dve.wait_ge(s["f_proj_done"], b + 1)
                    dve.tensor_tensor(z16[:, b, :], y0[:, b, :], bank[b % 3][:, 0:D], ALU.add)\
                        .then_inc(s["z_ready"], 1)
                if b >= 3:
                    z_rows(b - 3, 0, ln_rows[:, 1, :], y1, "y1_ready")
                if b < B:
                    z_stats(b, 0)
                if 2 <= b < B + 2:
                    z_scaled(b - 2, 0, ln_rows[:, 0, :])
                if b < B and b % 2:
                    pair_variance(b, 0)

            routed = [0]

            def route(ins):
                routed[0] += 1
                ins.then_inc(s["route_step"], 1)
                dve.wait_ge(s["route_step"], routed[0])

            logits = bank[6][:, 0:B * E].rearrange("p (b e) -> p b e", e=E)
            dve.wait_ge(s["logits_done"], B)
            route(dve.tensor_reduce(r_m[:, :], logits, AX.X, ALU.max))
            dve.tensor_tensor(r_a[:, :, :], logits, bcast(r_m), ALU.subtract).then_inc(s["shifted"], 1)
            route(dve.tensor_tensor(r_b[:, :, :], logits, bcast(r_m), ALU.is_equal))
            route(dve.tensor_tensor(r_b[:, :, :], r_b[:, :, :], rank[:, :, :], ALU.mult))
            route(dve.tensor_reduce(r_m[:, :], r_b[:, :, :], AX.X, ALU.max))
            dve.tensor_tensor(pick_bf[:, :, :], r_b[:, :, :], bcast(r_m), ALU.is_equal).then_inc(s["pick_ready"], 1)
            dve.wait_ge(s["gexp_ready"], 1)
            route(dve.tensor_reduce(r_s[:, :], lg[:, :, :], AX.X, ALU.add))
            dve.reciprocal(gate[:, :], r_s[:, :]).then_inc(s["gate_ready"], 1)
            dve.wait_ge(s["place_done"], 1)
            place = bank[7][:, 0:B * E].rearrange("p (b e) -> p b e", e=E)
            route(dve.tensor_scalar(r_b[:, :, :], place, float(CAP), None, ALU.is_lt))
            dve.tensor_tensor(kept[:, :, :], r_b[:, :, :], pick_bf[:, :, :], ALU.mult).then_inc(s["kept_ready"], 1)
            dve.wait_ge(s["gate_ready"], 1)
            dve.wait_ge(s["xb_ready"], 1)
            for m in range(B + 5):
                if m < B:
                    dve.wait_ge(s["hot_done"], m + 1)
                    if m >= 2:
                        dve.wait_ge(s["ffn_done"], m - 1)
                    dve.tensor_tensor(prod[:, m % 2, :, :], ps[:, 2 * (m % 2):2 * (m % 2) + 2, :]
                                      .rearrange("p a (e d) -> p (a e) d", d=D),
                                      y1T[:, m, :].unsqueeze(1).broadcast_to([128, E, D]), ALU.mult)\
                                          .then_inc(s["gated"], 1)
                b = m - 2
                if 0 <= b < B:
                    dve.wait_ge(s["ffn_done"], b + 1)
                    dve.scalar_tensor_tensor(z16[:, b, :], bank[4 + b % 4][:, 0:D], gate[:, b:b + 1], y1[:, b, :],
                                             ALU.mult, ALU.add).then_inc(s["z_ready"], 1)
                if m >= 5:
                    z_rows(m - 5, 1, x_sb[:, m - 5, :], y0, "out_rows")
                if 0 <= b < B:
                    z_stats(b, 1)
                if 4 <= m < B + 4:
                    z_scaled(m - 4, 1, ln_rows[:, 2, :])
                if 0 <= b < B and b % 2:
                    pair_variance(b, 1)

        @block.gpsimd
        def _(pool):
            pool.wait_ge(s["ones_ready"], 4)

            def subtract(c, j, u):
                pool.wait_ge(s["least_ready"], 4 * c + j + 1)
                pool.tensor_tensor(p_sb[:, u, j, :, :], p_sb[:, u, j, :, :],
                                   m_sb[:, u, j, :].unsqueeze(2).broadcast_to([128, QUADS, S]), ALU.subtract)\
                    .then_inc(s["subbed"], 1)

            def v_place_waits(c, layer):
                if layer_of(c, layer):
                    pool.wait_ge(s["kv_copied"], 2 * (c - B) + 2)
                else:
                    pool.wait_ge(s["v_copied"], c + 1)
                if late(c, 2):
                    pool.wait_ge(s["pv_done"], c - 1)

            def v_place(c, u, layer):
                v = kv_sb[:, c - B, 1, :] if layer_of(c, layer) else v_sb[:, :]
                pool.tensor_copy(vaug[:, u, :, 0:HD], v.rearrange("p (h d) -> p h d", d=HD))\
                    .then_inc(s["v_placed"], 1)

            def bucket_ctx(pair):
                if not isinstance(pair, int) or pair >= 1:
                    pool.wait_ge(s["kv_done"], 2 * pair)
                pool.tensor_tensor(cm[:, :, :], onehot[:, :, pair, :],
                                   ctx_sb[:, pair, :].unsqueeze(1).broadcast_to([128, NBUCKET, S]),
                                   ALU.mult).then_inc(s["cm_ready"], 1)

            def step(t, u, layer, pair):
                if late(t):
                    pool.wait_ge(s["veps_ready"], t + 1)
                    if late(t, 1):
                        pool.wait_ge(s["xn_ready"], t)
                    pool.tensor_tensor(rstd[:, :], veps[:, :], minus_half[:, :], ALU.pow)\
                        .then_inc(s["pow_done"], 1)
                if late(t - 2):
                    v_place_waits(t - 2, layer)
                if late(t - 2):
                    subtract(t - 2, 1, u)
                if late(t - 2):
                    v_place(t - 2, u, layer)
                if isinstance(t, int) and t < PEEL:
                    if t >= 2 and t < 5:
                        if t == 2:
                            pool.wait_ge(s["ctx_in"], 16)
                        pool.wait_ge(s["onehot_step"], NBUCKET)
                        bucket_ctx(t - 2)
                elif u == 0 and late(t):
                    if isinstance(t, int) or layer == 0:
                        pool.wait_ge(s["onehot_step"], 4 * NBUCKET)
                    bucket_ctx(pair)
                if isinstance(t, int) and t == T:
                    y0_power(0, B - 4, 1)
                if isinstance(t, int) and t == T + 2:
                    pool.wait_ge(s["split_done"], 2 * T)
                    pool.wait_ge(s["v_placed"], T)
                    pool.memset(kv_sb[:, :, :, :], 0.0).then_inc(s["kblk_zeroed"], 1)
                if late(t - 2):
                    subtract(t - 2, 3, u)
                if late(t) and layer_of(t, layer):
                    if isinstance(t, int) and t == B:
                        pool.wait_ge(s["xw_in"], 48)
                    pool.wait_ge(s["xn_ready"], t + 1)
                    rows = x_sb[:, batch(t, layer), :]
                    pool.tensor_tensor(rows, rows, bo_rows[:, :], ALU.add).then_inc(s["bo_added"], 1)

            def y0_power(b0, b1, n):
                pool.wait_ge(s["ve_ready"], n)
                pool.tensor_tensor(rs16[:, b0:b1], ve16[:, b0:b1], half16[:, b0:b1], ALU.pow)\
                    .then_inc(s["rs_ready"], 1)

            pipeline(pool, step)
            y0_power(B - 4, B, 2)
            pool.wait_ge(s["m_done"], 2)
            pool.memset(w1t_sb[:, :, :, :], 0.0).then_inc(s["kblk_zeroed"], 1)
            pool.wait_ge(s["ffn_w_in"], 16 * nloads[0])
            pool.wait_ge(s["y0_ready"], B)
            pool.tensor_tensor(x_sb[:, :, :], x_sb[:, :, :], ln_rows[:, 3, :].unsqueeze(1).broadcast_to([128, B, D]),
                               ALU.add).then_inc(s["xb_ready"], 1)
            pool.wait_ge(s["f_xT_done"], 4)
            pool.tensor_tensor(y0, y0, ob_rows[:, :].unsqueeze(1).broadcast_to([128, B, D]), ALU.add)\
                .then_inc(s["y0_biased"], 1)
            for n in range(B):
                p_unit = p_sb[:, (n // 4) % 2, n % 4, :, :]
                pool.wait_ge(s["f_drec"], n + 1)
                pool.tensor_tensor(p_unit, p_unit, drec[:, n, :].unsqueeze(2).broadcast_to([128, QUADS, 128]),
                                   ALU.mult)\
                    .then_inc(s["f_divided"], 1)

            def powers(k):
                for i in range(B // 2):
                    pool.wait_ge(s["ve_ready"], 2 + k * (B // 2) + i + 1)
                    pool.tensor_tensor(rs16[:, 2 * i:2 * i + 2], ve16[:, 2 * i:2 * i + 2], half16[:, 0:2], ALU.pow)\
                        .then_inc(s["rs_ready"], 1)

            powers(0)
            pool.wait_ge(s["crep_copied"], 1)
            pool.wait_ge(s["f_pT_done"], B)
            pool.tensor_tensor(cblk, crep[:, :].unsqueeze(1).broadcast_to([128, B, D]),
                               batchof[:, :].unsqueeze(2).broadcast_to([128, B, D]), ALU.mult)\
                                   .then_inc(s["cblk_ready"], 1)
            powers(1)

        @block.scalar
        def _(act):
            act.wait_ge(s["ones_ready"], 4)

            def exp_unit(c, j, u):
                if j % 2:
                    act.wait_ge(s["subbed"], 2 * c + j // 2 + 1)
                    act.activation(p_sb[:, u, j, :, :], p_sb[:, u, j, :, :], ACT.Exp, scale=-1.0)\
                       .then_inc(s["odd_exped"], 1)
                    return
                act.wait_ge(s["least_ready"], 4 * c + j + 1)
                for r in range(QUADS):
                    ins = act.activation(p_sb[:, u, j, r, :], quad[2 + j % 2][:, r, :], ACT.Exp,
                                         bias=m_sb[:, u, j, r:r + 1], scale=-1.0)
                ins.then_inc(s["even_exped"], 1)

            def pT_copy(p, j, u):
                act.wait_ge(s["pT_done"], 4 * p + j + 1)
                if j == 0 and late(p, 2):
                    act.wait_ge(s["pv_done"], p - 1)
                act.copy(pT[:, u, j, :, :], quad[4 + j % 2]).then_inc(s["pT_copied"], 1)

            def v_copy(h):
                act.wait_ge(s["split_done"], 2 * h + 2)
                if late(h, 1):
                    act.wait_ge(s["v_placed"], h)
                act.copy(v_sb[:, :], bank[0][:, 2 * D:3 * D]).then_inc(s["v_copied"], 1)

            def step(t, u, layer, pair):
                h, c, p, o = t - 1, t - 2, t - 3, t - 4
                if late(p):
                    exp_unit(p, 1, 1 - u)
                if late(o):
                    act.wait_ge(s["pv_done"], o + 1)
                    if late(o, 1):
                        act.wait_ge(s["o4_done"], o)
                    act.copy(oT[:, :, :], quad[6]).then_inc(s["oT_copied"], 1)
                if late(h):
                    act.wait_ge(s["xT_done"], h + 1)
                    if late(h, 1):
                        act.wait_ge(s["qkv_done"], h)
                    act.copy(xnT[:, :], bank[0][:, 384:512]).then_inc(s["xnT_copied"], 1)
                if late(p):
                    pT_copy(p, 0, 1 - u)
                if late(p):
                    pT_copy(p, 1, 1 - u)
                if late(c):
                    exp_unit(c, 0, u)
                if late(o):
                    act.wait_ge(s["fT_done"], o + 1)
                    if late(o, 1):
                        act.wait_ge(s["proj_done"], o)
                    act.copy(ofT[:, :], bank[1][:, 0:128]).then_inc(s["fT_copied"], 1)
                if late(p):
                    exp_unit(p, 3, 1 - u)
                if late(h):
                    act.wait_ge(s["q4T_done"], h + 1)
                    if late(h, 2):
                        act.wait_ge(s["s_done"], 4 * h - 4)
                    act.copy(q4[:, 1 - u, :, :], quad[1]).then_inc(s["q4_copied"], 1)
                if late(p):
                    pT_copy(p, 2, 1 - u)
                if late(p):
                    pT_copy(p, 3, 1 - u)
                if late(h) and layer_of(h, layer) == 0:
                    v_copy(h)
                if late(c):
                    exp_unit(c, 2, u)
                for k in kv_halves(t):
                    act.wait_ge(s["kv_done"], k + 1)
                    where = (k // 2, k % 2) if isinstance(k, int) else (pair - 1 + u, 1 - u)
                    act.copy(kv_sb[:, where[0], where[1], :], bank[7][:, 0:D]).then_inc(s["kv_copied"], 1)
                if isinstance(t, int) and t > T:
                    y0T_copy(t - T - 1)
                if isinstance(t, int) and t == T + 3:
                    expert_copy(0)

            def y0T_copy(i):
                act.wait_ge(s["cm_ready"], B)
                act.wait_ge(s["f_xT_done"], i + 1)
                act.copy(y0T.rearrange("p b s -> p (b s)").rearrange("p (g b j) -> p b g j", b=B, j=NPOS)
                         [:, 4 * i:4 * i + 4],
                         bank[0].rearrange("p (b g j) -> p b g j", b=4, j=NPOS)).then_inc(s["f_xT_copied"], 1)

            def expert_copy(i):
                act.wait_ge(s["m_done"], i + 1)
                act.copy(mexp[:, 4 * i:4 * i + 4, :], quad[2 + i]).then_inc(s["m_copied"], 1)

            pipeline(act, step)
            expert_copy(1)
            y0T_copy(3)
            act.wait_ge(s["ffn_w_in"], 16 * nloads[0])
            act.wait_ge(s["w_ffq_ready"], 2)
            for i in range(4):
                act.wait_ge(s["qk_done"], 2 * i + 1)
                act.activation(qT[:, 4 * i:4 * i + 4, :], quad[2 * (i % 2)], ACT.Identity, bias=inb_col[:, 0:1])\
                   .then_inc(s["qT_ready"], 1)
                rows = slice(MHD * (MH - 1), MHD * MH)
                act.wait_ge(s["qk_done"], 2 * i + 2)
                if i % 2 == 0:
                    act.wait_ge(s["kblk_zeroed"], i // 2 + 1)
                act.activation(kblk(rows, 4 * i, 4)[:, :, MH - 1, :], quad[2 * (i % 2) + 1][rows], ACT.Identity,
                               bias=inb_col[rows, 1:2]).then_inc(s["k_last_ready"], 1)
                act.wait_ge(s["v_done"], i + 1)
                act.copy(vM[:, 4 * i:4 * i + 4, :], quad[4 + i]).then_inc(s["v_ready"], 1)

            for m in range(B + 4):
                if m < B:
                    act.wait_ge(s["f_least_ready"], m + 1)
                    for r in range(QUADS):
                        ins = act.activation(p_sb[:, (m // 4) % 2, m % 4, r, :], quad[m % 4][:, r, :], ACT.Exp,
                                             bias=m_sb[:, (m // 4) % 2, m % 4, r:r + 1], scale=-1.0)
                    ins.then_inc(s["f_exped"], 1)
                n = m - 3
                if 0 <= n < B:
                    act.wait_ge(s["f_pT_done"], n + 1)
                    if n >= 8:
                        act.wait_ge(s["f_pv_done"], n - 7)
                    act.copy(pT[:, (n // 4) % 2, n % 4, :, :], quad[4 + n % 2]).then_inc(s["f_pT_copied"], 1)
                n = m - 4
                if n >= 0 and n % 4 == 3:
                    i = n // 4
                    act.wait_ge(s["f_pv_done"], n + 1)
                    act.activation(aT[:, :, 4 * NPOS * i:4 * NPOS * (i + 1)]
                                   .rearrange("p b (r j) -> p r b j", r=QUADS),
                                   quad[6 + i % 2].rearrange("p r (b j) -> p r b j", j=NPOS), ACT.Identity,
                                   bias=inb_col[:, 2:3]).then_inc(s["aT_ready"], 1)
            for b in range(B):
                act.wait_ge(s["y1T_done"], b + 1)
                act.copy(y1T[:, b, :], bank[4 + b % 2][:, 0:128]).then_inc(s["y1T_copied"], 1)
                if b in (1, 9):
                    half = b // 9
                    act.wait_ge(s["cb_done"], half + 1)
                    act.copy(b1w2[0:E, 4 * half:4 * half + 4, :], quad[7 - 4 * half][0:E])\
                        .then_inc(s["b1w2_ready"], 1)
                if b == 12:
                    act.wait_ge(s["crep_done"], 1)
                    act.copy(crep[:, :], bank[7][:, 0:128]).then_inc(s["crep_copied"], 1)
            act.wait_ge(s["shifted"], 1)
            act.activation(lg[:, :, :], r_a[:, :, :], ACT.Exp).then_inc(s["gexp_ready"], 1)
            act.wait_ge(s["keptT_done"], 1)
            act.copy(keptT_bf[:, :], bank[4][:, 0:128]).then_inc(s["keptT_copied"], 1)
            act.copy(keptT[:, :], bank[4][:, 0:128]).then_inc(s["keptT_copied"], 1)

        @block.tensor
        def _(pe):
            pe.wait_ge(s["ident_in"], 16)
            pe.wait_ge(s["ones_ready"], 4)

            def s_unit(c, j, u):
                if j == 0:
                    pe.wait_ge(s["q4_copied"], c + 1)
                    pe.wait_ge(s["k4_copied"], c + 1)
                if late(c, 1) or j >= 2:
                    if j % 2:
                        pe.wait_ge(s["least_ready"], 4 * c + j - 1)
                    else:
                        pe.wait_ge(s["even_exped"], 2 * c + j // 2)
                rows = slice(64 * (j // 2), 64 * (j // 2) + 64)
                for a in range(2):
                    r = 2 * (j % 2) + a
                    mm = pe.matmul(quad[2 + j % 2][:, 2 * a:2 * a + 2, :], q4[rows, u, r, :], k4[rows, u, r, :, :],
                                   start=True, stop=True)
                mm.then_inc(s["s_done"], 1)

            def pT_unit(p, j, u):
                pe.wait_ge(s["odd_exped" if j % 2 else "even_exped"], 2 * p + j // 2 + 1)
                if late(p, 1) or j >= 2:
                    pe.wait_ge(s["pT_copied"], 4 * p + j - 1)
                for r in range(QUADS):
                    mm = pe.transpose(bank[4 + j % 2][:, r * S:(r + 1) * S], p_sb[:, u, j, r, :], ident[:, :])
                mm.then_inc(s["pT_done"], 1)

            def project(h, u, layer):
                pe.wait_ge(s["xnT_copied"], h + 1)
                if isinstance(h, int) and h % B == 0:
                    pe.wait_ge(s["wq_ready"], h // B + 1)
                if layer_of(h, layer) == 0:
                    pe.matmul(bank[0][:, 0:3 * D], xnT[:, :], w_qkv_sb[:, :], start=True, stop=True)\
                      .then_inc(s["qkv_done"], 1)
                else:
                    pe.matmul(bank[0][:, 0:D], xnT[:, :], wq_sb[:, :], start=True, stop=True)\
                      .then_inc(s["qkv_done"], 1)

            def buckets_kv(k, t, u, pair, e0, e1):
                part, cm_pair = (k % 2, k // 2 + 1) if isinstance(k, int) else (1 - u, pair + u)
                if e0 == 0:
                    if isinstance(k, int) and k == 0:
                        pe.wait_ge(s["wkv_in"], 16)
                    pe.wait_ge(s["cm_ready"], cm_pair)
                    if late(t, 4):
                        pe.wait_ge(s["o_ready"], t - 3)
                    if isinstance(k, int) and k in (1, 3):
                        pe.wait_ge(s["kv_copied"], k)
                for e in range(e0, e1):
                    mm = pe.matmul(bank[7][:, 0:D], cm[:, e, :], wkv_sb[:, e, part * D:(part + 1) * D],
                                   start=(e == 0), stop=(e == NBUCKET - 1))
                if e1 == NBUCKET:
                    mm.then_inc(s["kv_done"], 1)

            def step(t, u, layer, pair):
                h, c, p, o = t - 1, t - 2, t - 3, t - 4
                halves = kv_halves(t)
                if late(h):
                    pe.wait_ge(s["xn_ready"], h + 1)
                    if late(h, 1):
                        pe.wait_ge(s["split_done"], 2 * h)
                        pe.wait_ge(s["v_copied"], min(h, B) if isinstance(h, int) else B if layer else h)
                    pe.transpose(bank[0][:, 384:512], xn[:, :], ident[:, :]).then_inc(s["xT_done"], 1)
                if late(c):
                    s_unit(c, 0, u)
                if late(p):
                    pT_unit(p, 0, 1 - u)
                if late(p):
                    pT_unit(p, 1, 1 - u)
                if late(o):
                    pe.wait_ge(s["oT_copied"], o + 1)
                    if late(o, 1):
                        pe.wait_ge(s["kv_copied"], {4: 2, 5: 4}.get(t, min(h, T)) if isinstance(h, int) else h)
                    for r in range(QUADS):
                        mm = pe.transpose(quad[7][:, r, :], oT[:, r, :], ident[:, :])
                    mm.then_inc(s["o4_done"], 1)
                if late(h):
                    project(h, 1 - u, layer)
                if late(p):
                    pT_unit(p, 2, 1 - u)
                if late(o):
                    pe.wait_ge(s["o_ready"], o + 1)
                    if late(h, 1):
                        pe.wait_ge(s["k4_copied"], h)
                    pe.transpose(bank[1][:, 0:128], o_sb[:, :], ident[:, :]).then_inc(s["fT_done"], 1)
                if late(c):
                    s_unit(c, 1, u)
                if halves:
                    buckets_kv(halves[0], t, u, pair, 0, 4)
                if late(c):
                    s_unit(c, 2, u)
                if late(h):
                    pe.wait_ge(s["split_done"], 2 * h + 1)
                    if late(o):
                        pe.wait_ge(s["fT_copied"], o + 1)
                    if late(h, 1):
                        pe.wait_ge(s["k4_copied"], h)
                    for r in range(QUADS):
                        mm = pe.transpose(quad[1][:, r, :], qs[:, 4 * r:4 * r + 4, :, :, :]
                                          .rearrange("p j b a d -> p (j b a d)"), ident[:, :])
                    mm.then_inc(s["q4T_done"], 1)
                if late(p):
                    pT_unit(p, 3, 1 - u)
                if late(h):
                    pe.wait_ge(s["split_done"], 2 * h + 2)
                    pe.wait_ge(s["q4_copied"], h + 1)
                    for r in range(QUADS):
                        mm = pe.transpose(quad[1][:, r, :], ks[:, 4 * r:4 * r + 4, :, :, :]
                                          .rearrange("p j b a d -> p (j b a d)"), ident[:, :])
                    mm.then_inc(s["k4T_done"], 1)
                if late(o):
                    pe.wait_ge(s["fT_copied"], o + 1)
                    if isinstance(o, int) and o == 0:
                        pe.wait_ge(s["attn_w_in"], 16)
                    if isinstance(o, int) and o == B:
                        pe.wait_ge(s["xw_in"], 48)
                    lo = layer_of(o, layer)
                    pe.matmul(bank[6][:, 0:D], ofT[:, :], w_out_sb[:, lo, :], start=True, stop=True)\
                      .then_inc(s["proj_done"], 1)
                if late(c):
                    s_unit(c, 3, u)
                if halves:
                    buckets_kv(halves[0], t, u, pair, 4, NBUCKET)
                if late(p):
                    pe.wait_ge(s["pT_copied"], 4 * p + 4)
                    pe.wait_ge(s["v_placed"], p + 1)
                    if late(o):
                        pe.wait_ge(s["resid_done"], o + 1)
                    for r in range(QUADS):
                        for j in range(QUADS):
                            mm = pe.matmul(quad[6][32 * j:32 * j + 32, r, :], vaug[:, 1 - u, 4 * r + j, :],
                                           pT[:, 1 - u, 2 * (j // 2) + r // 2, 2 * (r % 2) + j % 2, :],
                                           start=True, stop=True, skip_group_check=True)
                    mm.then_inc(s["pv_done"], 1)
                for k in halves[1:]:
                    buckets_kv(k, t, u, pair, 0, NBUCKET)
                if isinstance(t, int) and t > T:
                    y0T_quad(t - T - 1)
                if isinstance(t, int) and t == T + 2:
                    pe.wait_ge(s["even_exped"], 2 * T)
                    pe.wait_ge(s["least_ready"], 4 * T)
                    experts(0)

            def y0T_quad(i):
                if i == 0:
                    pe.wait_ge(s["split_done"], 2 * T)
                else:
                    pe.wait_ge(s["f_xT_copied"], i)
                for b in range(4 * i, 4 * i + 4):
                    pe.wait_ge(s["y0_ready"], b + 1)
                    mm = pe.transpose(quad[0][:, b % 4, :], y0[:, b, :], ident[:, :])
                mm.then_inc(s["f_xT_done"], 1)

            def experts(i):
                if i == 0:
                    pe.wait_ge(s["ffn_w_in"], 16 * nloads[0])
                else:
                    pe.wait_ge(s["last_w2_in"], 16)
                for e in range(4 * i, 4 * i + 4):
                    for c in range(FC):
                        mm = pe.matmul(quad[2 + i][:, e % 4, :], w1t_sb[:, e, c, :], w2_sb[:, e, c, :],
                                       start=(c == 0), stop=(c == FC - 1))
                mm.then_inc(s["m_done"], 1)

            pipeline(pe, step)
            experts(1)
            y0T_quad(3)
            pe.wait_ge(s["f_xT_copied"], 4)
            pe.wait_ge(s["m_copied"], 2)
            pe.wait_ge(s["w_ffq_ready"], 2)
            for i in range(4):
                if i >= 2:
                    pe.wait_ge(s["qT_ready"], i - 1)
                    pe.wait_ge(s["k_ready"], 3 * (i - 1))
                    pe.wait_ge(s["k_last_ready"], i - 1)
                for a in range(2):
                    pe.matmul(bank[2 * (i % 2) + a], inw_sb[:, a * D:(a + 1) * D], y0T[:, 4 * i:4 * i + 4, :],
                              start=True, stop=True).then_inc(s["qk_done"], 1)
                if i == 0:
                    pe.wait_ge(s["pT_copied"], 4 * T)
                    pe.wait_ge(s["oT_copied"], T)
                    pe.wait_ge(s["resid_done"], T)
                for g in range(4 * i, 4 * i + 4):
                    mm = pe.matmul(quad[4 + i][:, g % 4, :], y0T[:, g, :], inw_sb[:, 2 * D:3 * D],
                                   start=True, stop=True)
                mm.then_inc(s["v_done"], 1)
            pe.wait_ge(s["qT_ready"], 4)
            pe.wait_ge(s["k_ready"], 12)
            pe.wait_ge(s["k_last_ready"], 4)
            pe.wait_ge(s["v_ready"], 4)
            for m in range(B + 4):
                if m < B:
                    if m >= 4:
                        pe.wait_ge(s["f_exped"], m - 3)
                    pe.matmul(quad[m % 4], ident_bf[:, :], samepos[:, :].unsqueeze(1).broadcast_to([128, QUADS, 128]),
                              start=True, stop=False, skip_group_check=True)
                    pe.matmul(quad[m % 4], qT[:, m, :], kblk(slice(0, 128), m, 1)[:, 0], start=False, stop=True,
                              skip_group_check=True).then_inc(s["f_s_done"], 1)
                n = m - 3
                if 0 <= n < B:
                    pe.wait_ge(s["f_divided"], n + 1)
                    if n >= 2:
                        pe.wait_ge(s["f_pT_copied"], n - 1)
                    for r in range(QUADS):
                        mm = pe.transpose(quad[4 + n % 2][:, r, :], p_sb[:, (n // 4) % 2, n % 4, r, :], ident[:, :])
                    mm.then_inc(s["f_pT_done"], 1)
                n = m - 4
                if n >= 0:
                    i = n // 4
                    pe.wait_ge(s["f_pT_copied"], n + 1)
                    if i >= 2:
                        pe.wait_ge(s["aT_ready"], i - 1)
                    for j in range(MH):
                        mm = pe.matmul(quad[6 + i % 2][MHD * j:MHD * (j + 1), n % 4, :],
                                       vM[:, n, MHD * j:MHD * (j + 1)], pT[:, i % 2, n % 4, j, :],
                                       start=True, stop=True, skip_group_check=True)
                    mm.then_inc(s["f_pv_done"], 1)
            pe.wait_ge(s["aT_ready"], 4)
            for m in range(B + 6):
                if m < B:
                    if m >= 3:
                        pe.wait_ge(s["z_ready"], m - 2)
                    pe.matmul(bank[m % 3][:, 0:D], aT[:, m, :], ow_sb[:, :], start=True, stop=True)\
                      .then_inc(s["f_proj_done"], 1)
                if m % 2 == 0 and m < 4 * FC:
                    half, c = divmod(m // 2, FC)
                    mm = pe.matmul(quad[7 - 4 * half][0:E], b1t_sb[:, c, :], w2_sb[:, 4 * half:4 * half + 4, c, :],
                                   start=(c == 0), stop=(c == FC - 1))
                    if c == FC - 1:
                        mm.then_inc(s["cb_done"], 1)
                if m == 16:
                    pe.wait_ge(s["b1w2_ready"], 2)
                    for e in range(E):
                        pe.matmul(bank[7][:, 0:128], pick_expert[:, e, :], b1w2[0:E, e, :],
                                  start=(e == 0), stop=False)
                    pe.matmul(bank[7][:, 0:128], pick_all[:, :], b2_sb[:, :], start=False, stop=True)\
                      .then_inc(s["crep_done"], 1)
                b = m - 5
                if 0 <= b < B:
                    if b >= 2:
                        pe.wait_ge(s["y1T_copied"], b - 1)
                    pe.wait_ge(s["y1_ready"], b + 1)
                    pe.transpose(bank[4 + b % 2][:, 0:128], y1[:, b, :], ident[:, :]).then_inc(s["y1T_done"], 1)
                b = m - 6
                if b >= 0:
                    pe.wait_ge(s["y1T_copied"], b + 1)
                    pe.matmul(bank[6][:, b * E:(b + 1) * E], y1T[:, b, :], wg_sb[:, :], start=True, stop=True)\
                      .then_inc(s["logits_done"], 1)
            pe.wait_ge(s["pick_ready"], 1)
            pe.wait_ge(s["crep_copied"], 1)
            picks = pick_bf[:, :, :].rearrange("p b e -> p (b e)")
            pe.matmul(bank[7][:, 0:B * E], before[:, :], picks, start=True, stop=False, skip_group_check=True)
            for k in range(1, B):
                mm = pe.matmul(bank[7][:, k * E:B * E], ones_bf[:, :], picks[:, 0:(B - k) * E],
                               start=False, stop=(k == B - 1), skip_group_check=True)
            mm.then_inc(s["place_done"], 1)
            pe.wait_ge(s["kept_ready"], 1)
            pe.transpose(bank[4][:, 0:128], kept[:, :, :].rearrange("p b e -> p (b e)"), ident[:, :])\
                .then_inc(s["keptT_done"], 1)
            pe.wait_ge(s["keptT_copied"], 2)
            pe.wait_ge(s["cblk_ready"], 1)
            for m in range(B + 1):
                if m < B:
                    if m >= 2:
                        pe.wait_ge(s["gated"], m - 1)
                    for e in range(E):
                        row = m * E + e
                        mm = pe.matmul(quad[2 * (m % 2) + e // 4][:, e % 4, :],
                                       ident_bf[:, row:row + 1].broadcast_to([128, 128]), keptT_bf[:, :],
                                       start=True, stop=True)
                    mm.then_inc(s["hot_done"], 1)
                b = m - 1
                if b >= 0:
                    pe.wait_ge(s["gated"], b + 1)
                    if b >= 4:
                        pe.wait_ge(s["z_ready"], B + b - 3)
                    for e in range(E):
                        pe.matmul(bank[4 + b % 4][:, 0:D], prod[:, b % 2, e, :], mexp[:, e, :],
                                  start=(e == 0), stop=False)
                    pe.matmul(bank[4 + b % 4][:, 0:D], keptT[:, :], cblk[:, b, :], start=False, stop=True)\
                      .then_inc(s["ffn_done"], 1)


def kernel(**inputs):
    import numpy as _np
    import concourse.bacc as _bacc
    from concourse import mybir as _mybir
    from concourse.bass_utils import run_bass_kernel_spmd as _run

    a = {k: _np.asarray(v) for k, v in inputs.items()}
    import ml_dtypes
    bf = ml_dtypes.bfloat16
    p = _np.arange(128)
    arrays = {
        "x": a["x"],
        "ctxT": a["ctx_1024"].transpose(0, 2, 1),
        "fside": a["fside_BxS2_0"],
        "fsideT": a["fside_BxS2_0"].T,
        "itok": a["itok_BxS2_0_7"],
        "pad": a["mask_BxS2_bf0"].view(_np.int32),
        "w_qkv": a["L0_attn_w_qkv"],
        "w_out": a["L0_attn_w_out"],
        "wq": a["L0_xattn_Wq"],
        "wkv": _np.concatenate([a["L0_xattn_Wk_b"], a["L0_xattn_Wv_b"]], axis=2),
        "wo": a["L0_xattn_Wo"],
        "bo": a["L0_xattn_bo"],
        "inw": a["L0_ffn_in_proj_w"].T,
        "inb": a["L0_ffn_in_proj_b"].reshape(3, D).T,
        "ow": a["L0_ffn_out_proj_w"].T,
        "ob": a["L0_ffn_out_proj_b"],
        "g1": a["L0_ffn_ln1_g"],
        "be1": a["L0_ffn_ln1_b"],
        "g2": a["L0_ffn_ln2_g"],
        "be2": a["L0_ffn_ln2_b"],
        "wg": a["L0_ffn_wg"],
        "w1t": a["L0_ffn_w1"].transpose(0, 2, 1),
        "b1t": a["L0_ffn_b1"].T,
        "w2": a["L0_ffn_w2"],
        "b2": a["L0_ffn_b2"],
        "c_ident": _np.eye(128, dtype=_np.float32),
        "c_ident_bf": _np.eye(128, dtype=bf),
        "c_odd_even": (p[:, None] // 32 % 2 == _np.arange(2)[None, :]).astype(_np.float32),
        "c_causal": _np.where(p[:, None] >= p[None, :], 0.0, MASKED).astype(bf),
        "c_samepos": _np.where(p[:, None] % 8 == p[None, :] % 8, 0.0, MASKED).astype(bf),
        "c_before": (p[:, None] < p[None, :]).astype(bf),
        "c_rank": _np.broadcast_to(_np.arange(E, 0, -1, dtype=_np.float32), (128, B, E)),
        "c_batchof": (p[:, None] // E == _np.arange(B)[None, :]).astype(_np.float32),
    }
    rows = _np.eye(E)[:, None, None, :] * _np.eye(E)[:, :, None, None]
    rows = _np.concatenate([rows, rows.sum(axis=1, keepdims=True)], axis=1)
    arrays["c_pick_expert"] = _np.broadcast_to(rows, (E, E + 1, B, E)).reshape(E, E + 1, 128).astype(_np.float32)
    arrays = {k: _np.ascontiguousarray(v) for k, v in arrays.items()}
    nc = _bacc.Bacc("TRN2", target_bir_lowering=False, num_devices=1)
    args = {k: nc.dram_tensor(k, v.shape, _mybir.dt.from_np(v.dtype), kind="ExternalInput").ap()
            for k, v in arrays.items()}
    out = nc.dram_tensor("out", (B, S, D), _mybir.dt.float32, kind="ExternalOutput").ap()
    decoder_kernel(nc, **args, out=out)
    r = _run(nc, [arrays], core_ids=[0])
    return r.results[0]["out"]
```
